# Optimizing a Trainium2 kernel written in Bass

```python
import numpy as np
import jax
import jax.numpy as jnp

def _softmax(x, axis=-1):
    return jax.nn.softmax(x, axis=axis)

def _gelu(x):
    return jax.nn.gelu(x, approximate=True)

def _silu(x):
    return jax.nn.silu(x)

def _sigmoid(x):
    return jax.nn.sigmoid(x)

def _layernorm(x, axis=-1, eps=1e-05):
    m = jnp.mean(x, axis=axis, keepdims=True)
    v = jnp.var(x, axis=axis, keepdims=True)
    return (x - m) / jnp.sqrt(v + eps)

def _scatter_add(tgt, idx, src, axis=0):
    return tgt.at[idx].add(src)

def _segment_sum(src, seg, n):
    return jax.ops.segment_sum(src, seg, n)
kernel_name = 'mk_gnn_resnorm_d2_gnn_r32_cc3522'

def setup_inputs(seed: int=0):
    np.random.seed(seed)
    _w = jnp.asarray

    def _rec_inputs():
        import jax
        import jax.numpy as jnp
        _gk = jax.random.key(seed)
        x = -0.0005121 + 1.001 * jax.random.normal(jax.random.fold_in(_gk, 1), (3125, 16), jnp.float32)
        _s = jax.random.randint(jax.random.fold_in(_gk, 2), (50000,), 0, 3125, jnp.int32)
        _d = jax.random.randint(jax.random.fold_in(_gk, 3), (50000,), 0, 3125, jnp.int32)
        _loop = jnp.arange(3125, dtype=jnp.int32)
        src = jnp.concatenate([_s, _d, _loop])
        dst = jnp.concatenate([_d, _s, _loop])
        _o = jnp.argsort(dst, stable=True)
        src = src[_o]
        dst = dst[_o]
        edge_attr_16 = -0.00010739 + 0.99994 * jax.random.normal(jax.random.fold_in(_gk, 12), (103125, 16), jnp.float32)
        edge_type_90 = jax.random.randint(jax.random.fold_in(_gk, 14), (103125,), 0, 90, jnp.int32)
        return (x, src, dst, edge_attr_16, edge_type_90)
    x, src, dst, edge_attr_16, edge_type_90 = _rec_inputs()

    def _L0_gnn_setup():
        import jax, jax.numpy as jnp
        import numpy as np
        N_NODES = 6250
        N_EDGES = 100000
        F_IN = 16
        N_CLASSES = 16

        def _gin_conv(x, src, dst, eps, wa, ba, wb, bb, n_nodes):
            agg = jax.ops.segment_sum(x[src], dst, num_segments=n_nodes)
            h = (1.0 + eps) * x + agg
            h = jax.nn.relu(h @ wa + ba) @ wb + bb
            return h
        key = jax.random.key(seed)
        ks = jax.random.split(key, 8)
        s = 1.0 / np.sqrt(F_IN)
        return {'x': jax.random.normal(ks[0], (N_NODES, F_IN), dtype=jnp.float32), 'edge_index': jax.random.randint(ks[1], (2, N_EDGES), 0, N_NODES, dtype=jnp.int32), 'eps1': jnp.zeros((), dtype=jnp.float32), 'w1a': jax.random.normal(ks[2], (F_IN, 16), dtype=jnp.float32) * s, 'b1a': jnp.zeros((16,), dtype=jnp.float32), 'w1b': jax.random.normal(ks[3], (16, 16), dtype=jnp.float32) * 0.25, 'b1b': jnp.zeros((16,), dtype=jnp.float32), 'eps2': jnp.zeros((), dtype=jnp.float32), 'w2a': jax.random.normal(ks[4], (16, N_CLASSES), dtype=jnp.float32) * 0.25, 'b2a': jnp.zeros((N_CLASSES,), dtype=jnp.float32), 'w2b': jax.random.normal(ks[5], (N_CLASSES, N_CLASSES), dtype=jnp.float32) * 0.25, 'b2b': jnp.zeros((N_CLASSES,), dtype=jnp.float32)}
    _L0_gnn_all = _L0_gnn_setup()
    _L0_gnn_in = {k: v for k, v in _L0_gnn_all.items() if k in ('eps1', 'w1a', 'b1a', 'w1b', 'b1b', 'eps2', 'w2a', 'b2a', 'w2b', 'b2b')}
    del _L0_gnn_all

    def _L1_gnn_setup():
        import jax, jax.numpy as jnp
        import numpy as np
        N, E, IN, OUT, R, B = (50000, 25000, 16, 16, 90, 30)
        key = jax.random.key(seed)
        ks = jax.random.split(key, 9)
        h = jax.random.normal(ks[0], (N, IN), dtype=jnp.float32)
        he = jax.random.normal(ks[1], (E, IN), dtype=jnp.float32)
        Ws = jax.random.normal(ks[2], (OUT, IN), dtype=jnp.float32) * 0.1
        Wa = jax.random.normal(ks[3], (1, 3 * OUT), dtype=jnp.float32) * 0.1
        weight = jax.random.normal(ks[4], (B, IN, OUT), dtype=jnp.float32) * 0.1
        w_comp = jax.random.normal(ks[5], (R, B), dtype=jnp.float32) * 0.1
        src = jax.random.randint(ks[6], (E,), 0, N)
        dst = jax.random.randint(ks[7], (E,), 0, N)
        rel_type = jax.random.randint(ks[8], (E,), 0, R)
        return {'h': h, 'he': he, 'Ws': Ws, 'Wa': Wa, 'weight': weight, 'w_comp': w_comp, 'src': src, 'dst': dst, 'rel_type': rel_type}
    _L1_gnn_all = _L1_gnn_setup()
    _L1_gnn_in = {k: v for k, v in _L1_gnn_all.items() if k in ('Ws', 'Wa', 'weight', 'w_comp')}
    del _L1_gnn_all
    return {'x': x, 'src': src, 'dst': dst, 'edge_attr_16': edge_attr_16, 'edge_type_90': edge_type_90, 'L0_gnn_eps1': _L0_gnn_in['eps1'], 'L0_gnn_w1a': _L0_gnn_in['w1a'], 'L0_gnn_b1a': _L0_gnn_in['b1a'], 'L0_gnn_w1b': _L0_gnn_in['w1b'], 'L0_gnn_b1b': _L0_gnn_in['b1b'], 'L0_gnn_eps2': _L0_gnn_in['eps2'], 'L0_gnn_w2a': _L0_gnn_in['w2a'], 'L0_gnn_b2a': _L0_gnn_in['b2a'], 'L0_gnn_w2b': _L0_gnn_in['w2b'], 'L0_gnn_b2b': _L0_gnn_in['b2b'], 'L1_gnn_Ws': _L1_gnn_in['Ws'], 'L1_gnn_Wa': _L1_gnn_in['Wa'], 'L1_gnn_weight': _L1_gnn_in['weight'], 'L1_gnn_w_comp': _L1_gnn_in['w_comp']}

def reference(x, src, dst, edge_attr_16, edge_type_90, L0_gnn_eps1, L0_gnn_w1a, L0_gnn_b1a, L0_gnn_w1b, L0_gnn_b1b, L0_gnn_eps2, L0_gnn_w2a, L0_gnn_b2a, L0_gnn_w2b, L0_gnn_b2b, L1_gnn_Ws, L1_gnn_Wa, L1_gnn_weight, L1_gnn_w_comp):
    import jax
    import jax.numpy as jnp

    def _L0_gnn_ref(x, edge_index, eps1, w1a, b1a, w1b, b1b, eps2, w2a, b2a, w2b, b2b):
        import jax, jax.numpy as jnp
        import numpy as np
        N_NODES = 6250
        N_EDGES = 100000
        F_IN = 16
        N_CLASSES = 16

        def _gin_conv(x, src, dst, eps, wa, ba, wb, bb, n_nodes):
            agg = jax.ops.segment_sum(x[src], dst, num_segments=n_nodes)
            h = (1.0 + eps) * x + agg
            h = jax.nn.relu(h @ wa + ba) @ wb + bb
            return h
        src, dst = (edge_index[0], edge_index[1])
        n = x.shape[0]
        h = jax.nn.relu(_gin_conv(x, src, dst, eps1, w1a, b1a, w1b, b1b, n))
        h = _gin_conv(h, src, dst, eps2, w2a, b2a, w2b, b2b, n)
        return jax.nn.log_softmax(h, axis=1)

    def _L1_gnn_ref(h, he, Ws, Wa, weight, w_comp, src, dst, rel_type):
        import jax, jax.numpy as jnp
        import numpy as np
        N, E, IN, OUT, R, B = (50000, 25000, 16, 16, 90, 30)
        n_nodes, in_dim = h.shape
        num_bases, _, out_dim = weight.shape
        num_rels = w_comp.shape[0]
        V = weight.reshape(in_dim, num_bases, out_dim)
        W_rel = jnp.matmul(w_comp, V).reshape(num_rels, in_dim, out_dim)
        h_src = h[src]
        z_src = h_src @ Ws.T
        z_dst = h[dst] @ Ws.T
        z_e = he @ Ws.T
        e = jnp.concatenate([z_src, z_e, z_dst], axis=1) @ Wa.T
        msg = jnp.einsum('ei,eio->eo', h_src, W_rel[rel_type]) * e
        h_out = jax.ops.segment_sum(msg, dst, num_segments=n_nodes)
        return h_out
    edge_index = jnp.stack([src, dst])
    x = _layernorm(x + _L0_gnn_ref(x, edge_index, L0_gnn_eps1, L0_gnn_w1a, L0_gnn_b1a, L0_gnn_w1b, L0_gnn_b1b, L0_gnn_eps2, L0_gnn_w2a, L0_gnn_b2a, L0_gnn_w2b, L0_gnn_b2b), axis=-1)
    x = _layernorm(x + _L1_gnn_ref(x, edge_attr_16, L1_gnn_Ws, L1_gnn_Wa, L1_gnn_weight, L1_gnn_w_comp, src, dst, edge_type_90), axis=-1)
    return x

_drawn_inputs = setup_inputs


def setup_inputs(seed=0):
    import zlib

    import numpy as np

    out = dict(_drawn_inputs(seed))
    spreads = {'L0_gnn_b1a': (0.0, 0.8),
     'L0_gnn_b1b': (0.0, 0.573),
     'L0_gnn_b2a': (0.0, 2.0),
     'L0_gnn_b2b': (0.0, 2.0)}
    factors = {}
    for name, (base, spread) in spreads.items():
        noise = np.random.default_rng([zlib.crc32(name.encode()), seed]).standard_normal(out[name].shape)
        drawn = base * np.exp(spread * noise) if base else spread * noise
        out[name] = jnp.asarray(drawn.astype(out[name].dtype))
    for name, factor in factors.items():
        out[name] = (out[name] * factor).astype(out[name].dtype)
    return out
```

```python
import numpy as np
import concourse.bass as bass
import concourse.mybir as mybir
from contextlib import ExitStack

FP32 = mybir.dt.float32
BF16 = mybir.dt.bfloat16
FP16 = mybir.dt.float16
I32 = mybir.dt.int32
ALU = mybir.AluOpType
ACT = mybir.ActivationFunctionType
AX = mybir.AxisListType

P = 128
NODES, F = 3125, 16
EDGES = 103125
RELS, BASES = 90, 30
L = 8
B = 4
NODES_PAD = B * P * L
HI = -(-NODES // L)
FULL = NODES // (P * L)
LAST_P = (NODES - FULL * P * L) // L
LAST_L = NODES - FULL * P * L - LAST_P * L
TILES = -(-EDGES // P)
EDGE_BLOCKS = -(-TILES // P)
FULL_EB = TILES // P
LAST_T = EDGES // P - FULL_EB * P
LAST_E = EDGES - (FULL_EB * P + LAST_T) * P
CH = 13
CHUNKS = TILES // CH
assert CHUNKS * CH == TILES and CHUNKS % 2 == 0
PAD_DST = 8 * (HI + 100)
YW = F + 1
SLOTS = 6
KS = SLOTS * F
YCOLS = RELS * YW
YBANK = YCOLS // 3
EPS = 1e-5


def node_rows(dram, sb):
    top = FULL * P * L
    mid = top + LAST_P * L
    yield dram[0:top, :].rearrange("(b p l) f -> p b (l f)", p=P, l=L), sb[:, 0:FULL, :]
    yield dram[top:mid, :].rearrange("(p l) f -> p (l f)", l=L), sb[0:LAST_P, FULL, :]
    yield (dram[mid:NODES, :].rearrange("(a l) f -> a (l f)", a=1),
           sb[LAST_P:LAST_P + 1, FULL, 0:LAST_L * F])


def edge_rows(dram, sb, w):
    top = FULL_EB * P * P
    mid = top + LAST_T * P
    yield dram[0:top, :].rearrange("(b t e) w -> t b (e w)", t=P, e=P), sb[:, 0:FULL_EB, :]
    yield dram[top:mid, :].rearrange("(t e) w -> t (e w)", e=P), sb[0:LAST_T, FULL_EB, :]
    yield (dram[mid:EDGES, :].rearrange("(a e) w -> a (e w)", a=1),
           sb[LAST_T:LAST_T + 1, FULL_EB, 0:LAST_E * w])


def build_gnn(nc, x, src, dst, attr, etype, eps1, w1a, b1a, w1b, b1b, eps2, w2a, b2a, w2b, b2b,
              ws, wa, weight, w_comp, ident_c, iota_hi_c, lane_l_c, slot_c, out):
    h_tab = nc.dram_tensor("h_tab", [NODES_PAD, F], FP32, kind="Internal").ap()
    t_tab = nc.dram_tensor("t_tab", [F * RELS, F], FP32, kind="Internal").ap()
    y_tab = nc.dram_tensor("y_tab", [NODES_PAD * RELS, YW], FP32, kind="Internal").ap()

    ctx = ExitStack()
    with ctx:
        def sb(name, shape, dt=FP32):
            return ctx.enter_context(nc.sbuf_tensor(name, shape, dt))

        def sem(name):
            return ctx.enter_context(nc.semaphore(name))

        ident = sb("ident", [P, P])
        ident_bf = sb("ident_bf", [P, P], BF16)
        iota_hi = sb("iota_hi", [P, HI], FP16)
        iota_l = sb("iota_l", [P, L * F], FP16)
        slot_mask = sb("slot_mask", [KS, 3])
        zeros = sb("zeros", [P, HI + 1], BF16)
        kron = sb("kron", [P, 4, P])
        bias = sb("bias", [P, 4, F])
        eps = sb("eps", [P, 2])
        ws_sb = sb("ws_sb", [F, F])
        ws_rep = sb("ws_rep", [F, SLOTS, F])
        wa_sb = sb("wa_sb", [F, 3])
        wa_rep = sb("wa_rep", [F, 2, P])
        u_rows = sb("u_rows", [P, 2, F])
        u_src = sb("u_src", [KS, 1])
        comp_sb = sb("comp_sb", [RELS, BASES])
        compT = sb("compT", [BASES, RELS])
        v_sb = sb("v_sb", [BASES, F, F])
        t_sb = sb("t_sb", [RELS, F, F])
        w_full = sb("w_full", [KS, RELS, F])
        w_ext = sb("w_ext", [KS, RELS, YW])
        w_hi = sb("w_hi", [KS, YCOLS], BF16)
        w_mid = sb("w_mid", [KS, YCOLS], BF16)
        w_lo = sb("w_lo", [KS, YCOLS], BF16)
        w_stack = sb("w_stack", [KS, YCOLS], BF16)
        src_i = sb("src_i", [P, EDGE_BLOCKS, P], I32)
        dst_i = sb("dst_i", [P, EDGE_BLOCKS, P], I32)
        type_i = sb("type_i", [P, EDGE_BLOCKS, P], I32)
        hi_i = sb("hi_i", [P, EDGE_BLOCKS, P], I32)
        lo_i = sb("lo_i", [P, EDGE_BLOCKS, P], I32)
        raw = sb("raw", [P, 5, EDGE_BLOCKS * P])
        SRC, ROW, DHI, DLO, LOGIT = range(5)
        idx = sb("idx", [P, 2, EDGE_BLOCKS * P], I32)
        meta = sb("meta", [P, 3, EDGE_BLOCKS * P])
        attr_ring = sb("attr_ring", [P, 2, P * F])
        idx_st = sb("idx_st", [P, 2, CH], I32)
        meta_st = sb("meta_st", [P, 2, 3, CH])
        rows = sb("rows", [P, 2, CH, YW])
        msg = sb("msg", [P, CH, 2 * F])
        rest = sb("rest", [P, CH, 2 * F])
        part = [sb(f"part{k}", [P, CH, 2 * F], BF16) for k in range(3)]
        scale = sb("scale", [P, CH])
        oh_hi = sb("oh_hi", [P, 2, CH, HI + 1], BF16)
        oh_l = sb("oh_l", [P, CH, L * F], BF16)
        spread = sb("spread", [P, 2, CH, 6, L * F], BF16)
        xn = sb("xn", [P, B, L * F])
        hn = sb("hn", [P, B, L * F])
        x2n = sb("x2n", [P, B, L * F])
        agg_sb = sb("agg_sb", [P, 2, B * P])
        hT = sb("hT", [P, B, P])
        t1 = sb("t1", [P, B, L * F])
        t2 = sb("t2", [P, B, L * F])
        st1 = sb("st1", [P, B * L])
        st2 = sb("st2", [P, B * L])
        xs = sb("xs", [P, B * L, SLOTS, F], BF16)
        xsT = sb("xsT", [KS, B * L, P], BF16)
        y_sb = spread[:, :, :, :, :].rearrange("p a c q m -> p (a c q m)").bitcast(FP32)[
            :, 0:3 * YCOLS].rearrange("p (k w) -> p k w", k=3)

        PS = [ctx.enter_context(nc.psum_tensor(f"ps{k}", [P, 512], FP32)) for k in range(8)]

        s_const = sem("const_loaded")
        s_w = sem("weights_loaded")
        s_kron = sem("kron_loaded")
        s_x = sem("x_loaded")
        s_e = sem("edges_loaded")
        s_attr = [sem(f"attr_loaded{k}") for k in range(2)]
        s_attr_used = sem("attr_used")
        s_fill = sem("pads_filled")
        s_dve = sem("dve_step")
        s_pe = sem("pe_step")
        s_act = sem("act_step")
        s_t_out = sem("t_written")
        s_w_in = sem("w_rel_loaded")
        s_tab = sem("table_written")
        s_y_out = [sem(f"y_written{k}") for k in range(3)]
        s_out = sem("out_written")
        R = range(3)
        s_idx = [sem(f"idx_staged{r}") for r in R]
        s_meta = [sem(f"meta_staged{r}") for r in R]
        s_rows = [[sem(f"rows_landed{r}_{k}") for k in range(2)] for r in R]
        s_split = [sem(f"split_step{r}") for r in R]
        s_ready = [sem(f"operands_ready{r}") for r in R]
        s_used = [sem(f"operands_used{r}") for r in R]
        s_agg = sem("agg_done")
        s_begun = sem("gathers_begun")

        block = ctx.enter_context(nc.Block())

        @block.sync
        def _(sp):
            sp.wait_ge(s_fill, 4)
            for a, t in ((src, src_i), (dst, dst_i), (etype, type_i)):
                for d, s in edge_rows(a.rearrange("(e w) -> e w", w=1), t, 1):
                    sp.dma_start(s, d).then_inc(s_e, 16)
            sp.dma_start(ident[:, :], ident_c).then_inc(s_const, 16)
            sp.dma_start(iota_hi[:, :], iota_hi_c.partition_broadcast(P)).then_inc(s_const, 16)
            sp.dma_start(iota_l[:, :], lane_l_c.partition_broadcast(P)).then_inc(s_const, 16)
            sp.dma_start(slot_mask[:, :], slot_c).then_inc(s_const, 16)
            for d, s in node_rows(x, xn):
                sp.dma_start(s, d).then_inc(s_x, 16)
            top = FULL_EB * P * P
            for b in range(EDGE_BLOCKS):
                if b >= 2:
                    sp.wait_ge(s_attr_used, b - 1)
                o = attr_ring[:, b % 2, :]
                if b < FULL_EB:
                    sp.dma_start(o, attr[b * P * P:(b + 1) * P * P, :].rearrange(
                        "(t e) w -> t (e w)", e=P)).then_inc(s_attr[b % 2], 16)
                else:
                    mid = top + LAST_T * P
                    sp.dma_start(o[0:LAST_T, :], attr[top:mid, :].rearrange(
                        "(t e) w -> t (e w)", e=P)).then_inc(s_attr[b % 2], 16)
                    sp.dma_start(o[LAST_T:LAST_T + 1, 0:LAST_E * F], attr[mid:EDGES, :].rearrange(
                        "(a e) w -> a (e w)", a=1)).then_inc(s_attr[b % 2], 16)
            sp.wait_ge(s_act, A_TSB)
            sp.dma_start(t_tab.rearrange("(i r) o -> r i o", r=RELS), t_sb[:, :, :]).then_inc(s_t_out, 16)
            sp.wait_ge(s_t_out, 16)
            for k in range(SLOTS):
                sp.dma_start(w_full[k * F:(k + 1) * F, :, :],
                             t_tab.rearrange("(r i) o -> i r o", i=F)).then_inc(s_w_in, 16)
            sp.wait_ge(s_dve, D_H1)
            sp.dma_start(h_tab.rearrange("(b p l) f -> p b (l f)", p=P, l=L), hn[:, :, :]).then_inc(s_tab, 16)
            yv = y_tab.rearrange("(b p l r) w -> b l p (r w)", p=P, l=L, r=RELS)
            for c in range(B * L):
                sp.wait_ge(s_act, A_Y0 + c + 1)
                sp.wait_ge(s_dve, D_Y0 + c + 1)
                sp.dma_start(yv[c // L, c % L], y_sb[:, c % 3, :]).then_inc(s_y_out[c % 3], 16)
            sp.wait_ge(s_dve, D_OUT)
            for d, s in node_rows(out, t1):
                sp.dma_start(d, s).then_inc(s_out, 16)
            sp.wait_ge(s_out, 48)

        @block.gpsimd
        def _(pool):
            def gather(r, n, k, table, width):
                pool.wait_ge(s_idx[r], n + 1)
                if not isinstance(n, int) or n >= 2:
                    pool.wait_ge(s_ready[r], n - 1)
                pool.sem_inc(s_begun, 1)
                for j in range(CH):
                    pool.indirect_dma_start(
                        rows[:, k, j, 0:width], None, table,
                        bass.IndirectOffsetOnAxis(ap=idx_st[:, k, j:j + 1], axis=0),
                    ).then_inc(s_rows[r][k], 16)

            for r, (table, width) in enumerate(((x, F), (h_tab, F), (y_tab, YW))):
                if r == 1:
                    pool.wait_ge(s_tab, 16)
                if r == 2:
                    for k in range(3):
                        pool.wait_ge(s_y_out[k], 16 * len(range(k, B * L, 3)))
                gather(r, 0, 0, table, width)
                gather(r, 1, 1, table, width)
                with pool.Fori(2, CHUNKS, 2) as n:
                    gather(r, n, 0, table, width)
                    gather(r, n + 1, 1, table, width)

        @block.scalar
        def _(act):
            for k, a in enumerate((w1a, w1b, w2a, w2b)):
                if k == 0:
                    act.wait_ge(s_fill, 5)
                for l in range(L):
                    act.dma_start(kron[l * F:(l + 1) * F, k, l * F:(l + 1) * F], a).then_inc(s_kron, 16)
            for k, a in enumerate((b1a, b1b, b2a, b2b)):
                act.dma_start(bias[:, k, :], a.partition_broadcast(P)).then_inc(s_w, 16)
            for k, a in enumerate((eps1, eps2)):
                act.dma_start(eps[:, k:k + 1], a.partition_broadcast(P)).then_inc(s_w, 16)
            act.dma_start(ws_sb[:, :], ws).then_inc(s_w, 16)
            act.dma_start(wa_sb[:, :], wa.rearrange("a (k o) -> (a o) k", k=3),
                          allow_slow_non_contiguous=True).then_inc(s_w, 16)
            act.dma_start(comp_sb[:, :], w_comp).then_inc(s_w, 16)
            act.dma_start(v_sb[:, :, :], weight.rearrange("b i o -> (b i o)").rearrange(
                "(i b o) -> b i o", i=F, b=BASES)).then_inc(s_w, 16)

            step = [0]

            def done(ins):
                step[0] += 1
                ins.then_inc(s_act, 1)
                return step[0]

            for g, (dsts) in enumerate(EDGE_T):
                act.wait_ge(s_pe, P_EDGE + g + 1)
                done(nc.scalar.copy(dsts(idx, meta), PS[g % 2][:, 0:dsts.width]))
            assert step[0] == A_EDGE
            act.wait_ge(s_pe, P_U)
            done(nc.scalar.copy(u_rows[:, :, :], PS[2][:, 0:2 * F].rearrange("p (k f) -> p k f", k=2)))
            done(nc.scalar.copy(u_src[:, :], PS[2][0:KS, 64:65]))
            done(nc.scalar.copy(compT[:, :], PS[3][0:BASES, 0:RELS]))
            assert step[0] == A_COMP
            act.wait_ge(s_pe, P_T)
            done(nc.scalar.copy(t_sb[:, :, :], PS[3][0:RELS, 128:128 + F * F].rearrange(
                "r (i o) -> r i o", i=F)))
            assert step[0] == A_TSB

            def stage(r, n, k, which):
                if not isinstance(n, int) or n >= 2:
                    act.wait_ge(s_rows[r][k], 8 * CH * (n - k))
                act.copy(idx_st[:, k, :], idx[:, which, bass.ds(n * CH, CH)]).then_inc(s_idx[r], 1)
                if not isinstance(n, int) or n >= 2:
                    act.wait_ge(s_ready[r], n - 1)
                m = 2 + (r == 2)
                act.copy(meta_st[:, k, 0:m, :], meta[:, 0:m, bass.ds(n * CH, CH)]).then_inc(s_meta[r], 1)

            for r in R:
                if r == 0:
                    act.wait_ge(s_act, A_EDGE)
                if r:
                    act.wait_ge(s_ready[r - 1], CHUNKS)
                if r == 2:
                    act.wait_ge(s_dve, D_LOGIT)
                stage(r, 0, 0, r // 2)
                stage(r, 1, 1, r // 2)
                with act.Fori(2, CHUNKS, 2) as n:
                    stage(r, n, 0, r // 2)
                    stage(r, n + 1, 1, r // 2)
                if r == 1:
                    act.wait_ge(s_dve, D_SM)
                    done(nc.scalar.activation(t2[:, :, :], t1[:, :, :], ACT.Exp))
                    assert step[0] == A_EXP
                    act.wait_ge(s_dve, D_SUM)
                    done(nc.scalar.activation(st2[:, :], st1[:, :], ACT.Ln))
                    assert step[0] == A_LN
                    act.wait_ge(s_dve, D_VAR1)
                    done(nc.scalar.activation(st2[:, :], st1[:, :], ACT.Sqrt))
                    assert step[0] == A_SQ1
                    for c in range(B * L):
                        act.wait_ge(s_pe, P_Y0 + c + 1)
                        if c >= 3:
                            act.wait_ge(s_y_out[c % 3], 16 * (c // 3))
                        s = 2 + 3 * (c % 2)
                        if c % 2 == 0:
                            nc.scalar.copy(y_sb[:, c % 3, YBANK:2 * YBANK], PS[s + 1][:, 0:YBANK])
                        done(nc.scalar.copy(y_sb[:, c % 3, 0:YBANK], PS[s][:, 0:YBANK]))
                    assert step[0] == A_Y0 + B * L
            act.wait_ge(s_dve, D_VAR2)
            done(nc.scalar.activation(st2[:, :], st1[:, :], ACT.Sqrt))
            assert step[0] == A_SQ2

        @block.vector
        def _(dve):
            count = [0]

            def step(ins):
                count[0] += 1
                ins.then_inc(s_dve, 1)
                return count[0]

            def chain(ins):
                dve.wait_ge(s_dve, step(ins))

            v = nc.vector
            v.memset(dst_i[:, FULL_EB, :], PAD_DST).then_inc(s_fill, 1)
            v.memset(src_i[:, FULL_EB, :], 0).then_inc(s_fill, 1)
            v.memset(type_i[:, FULL_EB, :], 0).then_inc(s_fill, 1)
            v.memset(xn[:, FULL:, :], 0.0).then_inc(s_fill, 1)
            v.memset(kron[:, :, :], 0.0).then_inc(s_fill, 1)
            v.memset(agg_sb[:, :, HI:], 0.0)
            step(v.memset(zeros[:, :], 0.0))
            dve.wait_ge(s_e, 16 * 9)
            raw3 = [raw[:, k, :].rearrange("p (b e) -> p b e", b=EDGE_BLOCKS) for k in range(5)]
            chain(v.tensor_copy(raw3[SRC], src_i[:, :, :]))
            chain(v.tensor_scalar(raw3[ROW], raw3[SRC], float(RELS), None, ALU.mult))
            step(v.tensor_tensor(raw3[ROW], raw3[ROW], type_i[:, :, :], ALU.add))
            step(v.tensor_scalar(hi_i[:, :, :], dst_i[:, :, :], 3, None, ALU.arith_shift_right))
            chain(v.tensor_scalar(lo_i[:, :, :], dst_i[:, :, :], L - 1, None, ALU.bitwise_and))
            step(v.tensor_copy(raw3[DHI], hi_i[:, :, :]))
            step(v.tensor_copy(raw3[DLO], lo_i[:, :, :]))
            dve.wait_ge(s_const, 16 * 4)
            step(v.tensor_copy(ident_bf[:, :], ident[:, :]))
            dve.wait_ge(s_w, 16 * 10)
            step(v.tensor_copy(ws_rep[:, :, :], ws_sb[:, :].rearrange("o (a i) -> o a i", a=1)
                               .broadcast_to([F, SLOTS, F])))
            chain(v.tensor_copy(wa_rep[:, :, :], wa_sb[:, 1:3].rearrange("o (k a) -> o k a", a=1)
                               .broadcast_to([F, 2, P])))
            assert count[0] == D_PREP, count[0]
            chain(v.tensor_scalar(eps[:, :], eps[:, :], 1.0, None, ALU.add))

            dve.wait_ge(s_act, A_COMP)
            for b in range(EDGE_BLOCKS):
                dve.wait_ge(s_attr[b % 2], 16 * (b // 2 + 1) + 16 * (b == FULL_EB))
                a3 = attr_ring[:, b % 2, :].rearrange("p (e f) -> p e f", f=F)
                chain(v.tensor_tensor(a3, a3, u_rows[:, 0:1, :].broadcast_to([P, P, F]), ALU.mult))
                v.tensor_reduce(raw[:, LOGIT, b * P:(b + 1) * P], a3, AX.X, ALU.add).then_inc(s_attr_used, 1)
            assert count[0] == D_ATTR, count[0]
            dve.wait_ge(s_pe, P_LT)
            step(v.tensor_copy(meta[:, 2, 0:512], PS[4][:, :]))
            step(v.tensor_copy(meta[:, 2, 512:], PS[5][:, 0:EDGE_BLOCKS * P - 512]))
            assert count[0] == D_LOGIT, count[0]

            def edge_chunk(r, n, k):
                w = F if r < 2 else 2 * F
                steps = 4 if r < 2 else 6
                got, base = rows[:, k, :, :], 0

                def split(ins, i):
                    ins.then_inc(s_split[r], 1)
                    return n * steps + i + 1

                dve.wait_ge(s_meta[r], n + 1)
                if not isinstance(n, int) or n >= 2:
                    dve.wait_ge(s_used[r], n - 1)
                for j in range(CH):
                    v.tensor_scalar(oh_hi[:, k, j, 0:HI], iota_hi[:, :], meta_st[:, k, 0, j:j + 1],
                                    None, ALU.is_equal)
                if not isinstance(n, int) or n >= 1:
                    dve.wait_ge(s_ready[r], n)
                for j in range(CH):
                    v.tensor_scalar(oh_l[:, j, :], iota_l[:, :], meta_st[:, k, 1, j:j + 1],
                                    None, ALU.is_equal)
                dve.wait_ge(s_rows[r][k], 8 * CH * (n - k + 2))
                i = 0
                val = got[:, :, 0:F]
                if r == 2:
                    at = split(v.tensor_tensor(scale[:, :], got[:, :, F], meta_st[:, k, 2, :], ALU.add), 0)
                    dve.wait_ge(s_split[r], at)
                    v.tensor_tensor(msg[:, :, 0:F], val, scale[:, :].rearrange("p (c a) -> p c a", a=1)
                                    .broadcast_to([P, CH, F]), ALU.mult)
                    at = split(v.tensor_copy(msg[:, :, F:2 * F], val), 1)
                    dve.wait_ge(s_split[r], at)
                    val, i = msg[:, :, :], 2
                p0, p1, p2 = (q[:, :, 0:w] for q in part)
                rs = rest[:, :, 0:w]
                dve.wait_ge(s_split[r], split(v.tensor_copy(p0, val), i))
                dve.wait_ge(s_split[r], split(v.tensor_tensor(rs, val, p0, ALU.subtract), i + 1))
                dve.wait_ge(s_split[r], split(v.tensor_copy(p1, rs), i + 2))
                dve.wait_ge(s_split[r], split(v.tensor_tensor(p2, rs, p1, ALU.subtract), i + 3))
                oh4 = oh_l[:, :, :].rearrange("p c (l f) -> p c l f", f=F)
                for h in range(w // F):
                    for q in range(3):
                        o = spread[:, k, :, 3 * h + q, :].rearrange("p c (l f) -> p c l f", f=F)
                        s = part[q][:, :, h * F:(h + 1) * F].rearrange("p c (a f) -> p c a f", a=1)
                        last = v.tensor_tensor(o, oh4, s.broadcast_to([P, CH, L, F]), ALU.mult)
                last.then_inc(s_ready[r], 1)

            def edges(r):
                edge_chunk(r, 0, 0)
                edge_chunk(r, 1, 1)
                with dve.Fori(2, CHUNKS, 2) as n:
                    edge_chunk(r, n, 0)
                    edge_chunk(r, n + 1, 1)

            pe_at = [P_AGG0]

            def copy_t(halves):
                dve.wait_ge(s_agg, agg_n[0] + 1)
                agg_n[0] += 1
                for h in range(halves):
                    last = step(v.tensor_copy(agg_sb[:, h, 0:HI], PS[h][:, 0:HI]))
                pe_at[0] += 1
                dve.wait_ge(s_pe, pe_at[0])

            agg_n = [0]
            flat = lambda t: t[:, :, :].rearrange("p b (l f) -> p (b l) f", f=F)
            row = lambda s: s[:, :].rearrange("p (c a) -> p c a", a=1).broadcast_to([P, B * L, F])
            brow = lambda k: bias[:, k:k + 1, :].broadcast_to([P, B * L, F])

            def linear(k, src_t):
                pe_at[0] += 1
                dve.wait_ge(s_pe, pe_at[0])
                step(v.tensor_copy(hT[:, :, :], PS[4][:, :].rearrange("p (b n) -> p b n", b=B)))
                pe_at[0] += 1
                dve.wait_ge(s_pe, pe_at[0])
                chain(v.tensor_tensor(flat(t1), PS[3][:, :].rearrange("p (c f) -> p c f", f=F), brow(k), ALU.add))

            def layer_norm(o, i, a_sq, d_var):
                chain(v.tensor_reduce(st1[:, :], flat(i), AX.X, ALU.add))
                chain(v.tensor_scalar(st1[:, :], st1[:, :], 1.0 / F, None, ALU.mult))
                chain(v.tensor_tensor(flat(i), flat(i), row(st1), ALU.subtract))
                chain(v.tensor_tensor(flat(t2), flat(i), flat(i), ALU.mult))
                chain(v.tensor_reduce(st1[:, :], flat(t2), AX.X, ALU.add))
                step(v.tensor_scalar(st1[:, :], st1[:, :], 1.0 / F, EPS, ALU.mult, ALU.add))
                assert count[0] == d_var, count[0]
                dve.wait_ge(s_act, a_sq)
                chain(v.reciprocal(st2[:, :], st2[:, :]))
                chain(v.tensor_tensor(flat(o), flat(i), row(st2), ALU.mult))

            cur = xn
            for r in range(2):
                edges(r)
                copy_t(1)
                if r == 0:
                    dve.wait_ge(s_x, 48)
                chain(v.tensor_scalar(t2[:, :, :], cur[:, :, :], eps[:, r:r + 1], None, ALU.mult))
                chain(v.tensor_tensor(t1[:, :, :], t2[:, :, :],
                                      PS[2][:, :].rearrange("p (b c) -> p b c", b=B), ALU.add))
                assert count[0] == (D_GIN0 if r == 0 else D_GIN1), count[0]
                linear(2 * r, t1)
                chain(v.tensor_scalar(t1[:, :, :], t1[:, :, :], 0.0, None, ALU.max))
                assert count[0] == (D_LIN0 if r == 0 else D_LIN1), count[0]
                linear(2 * r + 1, t1)
                if r == 0:
                    step(v.tensor_scalar(hn[:, :, :], t1[:, :, :], 0.0, None, ALU.max))
                    assert count[0] == D_H1, count[0]
                    dve.wait_ge(s_dve, D_H1)
                    cur = hn
            chain(v.tensor_reduce(st1[:, :], flat(t1), AX.X, ALU.max))
            chain(v.tensor_tensor(flat(t1), flat(t1), row(st1), ALU.subtract))
            assert count[0] == D_SM, count[0]
            dve.wait_ge(s_act, A_EXP)
            step(v.tensor_reduce(st1[:, :], flat(t2), AX.X, ALU.add))
            assert count[0] == D_SUM, count[0]
            dve.wait_ge(s_act, A_LN)
            chain(v.tensor_tensor(flat(t1), flat(t1), row(st2), ALU.subtract))
            chain(v.tensor_tensor(t1[:, :, :], t1[:, :, :], xn[:, :, :], ALU.add))
            layer_norm(x2n, t1, A_SQ1, D_VAR1)
            x3 = flat(x2n)
            chain(v.tensor_copy(xs[:, :, 0, :], x3))
            chain(v.tensor_tensor(flat(t1), x3, xs[:, :, 0, :], ALU.subtract))
            chain(v.tensor_copy(xs[:, :, 3, :], flat(t1)))
            step(v.tensor_tensor(xs[:, :, 5, :], flat(t1), xs[:, :, 3, :], ALU.subtract))
            for s, o in ((0, 1), (0, 2), (3, 4)):
                step(v.tensor_copy(xs[:, :, o, :], xs[:, :, s, :]))
            dve.wait_ge(s_w_in, 16 * SLOTS)
            step(v.tensor_copy(w_ext[:, :, 0:F], w_full[:, :, :]))
            chain(v.tensor_copy(w_ext[:, :, F:YW], u_src[:, :].rearrange("p (a b) -> p a b", a=1)
                                .broadcast_to([KS, RELS, 1])))
            we = w_ext[:, :, :].rearrange("p r w -> p (r w)")
            chain(v.tensor_copy(w_hi[:, :], we))
            chain(v.tensor_tensor(we, we, w_hi[:, :], ALU.subtract))
            chain(v.tensor_copy(w_mid[:, :], we))
            chain(v.tensor_tensor(w_lo[:, :], we, w_mid[:, :], ALU.subtract))
            chain(v.tensor_scalar(w_stack[:, :], w_hi[:, :], slot_mask[:, 0:1], None, ALU.mult))
            chain(v.scalar_tensor_tensor(out=w_stack[:, :], in0=w_mid[:, :], scalar=slot_mask[:, 1:2],
                                         in1=w_stack[:, :], op0=ALU.mult, op1=ALU.add))
            step(v.scalar_tensor_tensor(out=w_stack[:, :], in0=w_lo[:, :], scalar=slot_mask[:, 2:3],
                                        in1=w_stack[:, :], op0=ALU.mult, op1=ALU.add))
            assert count[0] == D_XS, count[0]
            for g in range(B * L // 4):
                dve.wait_ge(s_pe, P_XT0 + g + 1)
                step(v.tensor_copy(xsT[:, 4 * g:4 * g + 4, :],
                                   PS[g % 2][:, :].bitcast(BF16)[0:KS, 0:4 * P].rearrange("k (c p) -> k c p", c=4)))
            assert count[0] == D_XT, count[0]
            for c in range(B * L):
                dve.wait_ge(s_pe, P_Y0 + c + 1)
                if c >= 3:
                    dve.wait_ge(s_y_out[c % 3], 16 * (c // 3))
                s = 2 + 3 * (c % 2)
                if c % 2:
                    v.tensor_copy(y_sb[:, c % 3, YBANK:2 * YBANK], PS[s + 1][:, 0:YBANK])
                step(v.tensor_copy(y_sb[:, c % 3, 2 * YBANK:], PS[s + 2][:, 0:YBANK]))
            assert count[0] == D_Y0 + B * L, count[0]
            chain(v.tensor_tensor(flat(t2), x3, u_rows[:, 1:2, :].broadcast_to([P, B * L, F]), ALU.mult))
            chain(v.tensor_reduce(st2[:, :], flat(t2), AX.X, ALU.add))
            edges(2)
            pe_at[0] = P_AGG2
            copy_t(2)
            ps3 = lambda k: PS[k][:, :].rearrange("p (c f) -> p c f", f=F)
            chain(v.tensor_tensor(flat(t1), ps3(3), row(st2), ALU.mult))
            chain(v.tensor_tensor(flat(t1), flat(t1), ps3(2), ALU.add))
            chain(v.tensor_tensor(t1[:, :, :], t1[:, :, :], x2n[:, :, :], ALU.add))
            layer_norm(t1, t1, A_SQ2, D_VAR2)
            assert count[0] == D_OUT, count[0]

        @block.tensor
        def _(pe):
            count = [0]

            def step(ins):
                count[0] += 1
                ins.then_inc(s_pe, 1)

            mm, tr = nc.tensor.matmul, nc.tensor.transpose
            pe.wait_ge(s_dve, D_PREP)
            for g, t in enumerate(EDGE_T):
                if g >= 2:
                    pe.wait_ge(s_act, g - 1)
                for q in range(t.width // P):
                    last = tr(PS[g % 2][:, q * P:(q + 1) * P], raw[:, t.raw, t.at + q * P:t.at + (q + 1) * P],
                              ident[:, :])
                step(last)
            assert count[0] == P_EDGE + len(EDGE_T)
            mm(PS[2][:, 0:F], wa_rep[:, 0, :], ws_sb[:, :], start=True, stop=True)
            mm(PS[2][:, F:2 * F], wa_rep[:, 1, :], ws_sb[:, :], start=True, stop=True)
            mm(PS[2][0:KS, 64:65], ws_rep[:, :, :].rearrange("o s i -> o (s i)"), wa_sb[:, 0:1],
               start=True, stop=True)
            step(tr(PS[3][0:BASES, 0:RELS], comp_sb[:, :], ident[0:RELS, 0:RELS]))
            assert count[0] == P_U
            pe.wait_ge(s_act, A_COMP)
            step(mm(PS[3][0:RELS, 128:128 + F * F], compT[:, :], v_sb[:, :, :].rearrange("b i o -> b (i o)"),
                    start=True, stop=True))
            assert count[0] == P_T
            for b in range(EDGE_BLOCKS):
                pe.wait_ge(s_attr_used, b + 1)
                last = tr(PS[4 + b // 4][:, (b % 4) * P:(b % 4 + 1) * P], raw[:, LOGIT, b * P:(b + 1) * P],
                          ident[:, :])
            step(last)
            assert count[0] == P_LT

            def edges(r):
                halves = 1 if r < 2 else 2
                for h in range(halves):
                    mm(PS[h][:, 0:HI], zeros[:, 0:P], zeros[:, 0:HI], start=True, stop=False)

                def chunk(n, k):
                    pe.wait_ge(s_ready[r], n + 1)
                    for j in range(CH):
                        for h in range(halves):
                            for q in range(3):
                                last = mm(PS[h][:, 0:HI], spread[:, k, j, 3 * h + q, :], oh_hi[:, k, j, 0:HI],
                                          start=False, stop=False)
                    last.then_inc(s_used[r], 1)

                with pe.Fori(0, CHUNKS, 2) as n:
                    chunk(n, 0)
                    chunk(n + 1, 1)
                for h in range(halves):
                    last = mm(PS[h][:, 0:HI], zeros[:, 0:P], zeros[:, 0:HI], start=False, stop=True)
                last.then_inc(s_agg, 1)

            def to_nodes(halves, d):
                pe.wait_ge(s_dve, d)
                for h in range(halves):
                    for b in range(B):
                        last = tr(PS[2 + h][:, b * P:(b + 1) * P], agg_sb[:, h, b * P:(b + 1) * P], ident[:, :])
                step(last)

            def linear(k, d):
                pe.wait_ge(s_dve, d)
                for b in range(B):
                    last = tr(PS[4][:, b * P:(b + 1) * P], t1[:, b, :], ident[:, :])
                step(last)
                pe.wait_ge(s_dve, d + 1)
                for b in range(B):
                    last = mm(PS[3][:, b * P:(b + 1) * P], hT[:, b, :], kron[:, k, :], start=True, stop=True)
                step(last)

            assert count[0] == P_AGG0
            pe.wait_ge(s_dve, 1)
            pe.wait_ge(s_act, A_EDGE)
            pe.wait_ge(s_kron, 16 * 32)
            for r in range(2):
                edges(r)
                to_nodes(1, (D_GIN0, D_GIN1)[r] - 2)
                linear(2 * r, (D_GIN0, D_GIN1)[r])
                linear(2 * r + 1, (D_LIN0, D_LIN1)[r])
            pe.wait_ge(s_dve, D_XS)
            assert count[0] == P_XT0
            for g in range(B * L // 4):
                if g >= 2:
                    pe.wait_ge(s_dve, D_XS + g - 1)
                for q in range(4):
                    c = 4 * g + q
                    last = tr(PS[g % 2][:, :].bitcast(BF16)[0:KS, q * P:(q + 1) * P],
                              xs[:, c, :, :].rearrange("p s f -> p (s f)"), ident_bf[:, :])
                step(last)
            pe.wait_ge(s_dve, D_XT)
            assert count[0] == P_Y0
            for c in range(B * L):
                if c >= 2:
                    pe.wait_ge(s_act, A_Y0 + c - 1)
                    pe.wait_ge(s_dve, D_Y0 + c - 1)
                for q in range(3):
                    last = mm(PS[2 + 3 * (c % 2) + q][:, 0:YBANK], xsT[:, c, :],
                              w_stack[:, q * YBANK:(q + 1) * YBANK], start=True, stop=True)
                step(last)
            assert count[0] == P_AGG2
            edges(2)
            to_nodes(2, D_OUT - 3 - 8)


class Group:

    def __init__(self, raw, at, width, into):
        self.raw, self.at, self.width, self.into = raw, at, width, into

    def __call__(self, idx, meta):
        kind, k = self.into
        return (idx if kind == "idx" else meta)[:, k, self.at:self.at + self.width]


EDGE_COLS = EDGE_BLOCKS * P
EDGE_T = [Group(k, at, min(512, EDGE_COLS - at), into)
          for k, into in enumerate((("idx", 0), ("idx", 1), ("meta", 0), ("meta", 1)))
          for at in range(0, EDGE_COLS, 512)]

P_EDGE = 0
P_U = P_EDGE + len(EDGE_T) + 1
P_T = P_U + 1
P_LT = P_T + 1
P_AGG0 = P_LT
P_XT0 = P_AGG0 + 2 * 5
P_Y0 = P_XT0 + B * L // 4
P_AGG2 = P_Y0 + B * L
A_EDGE = len(EDGE_T)
A_COMP = A_EDGE + 3
A_TSB = A_COMP + 1
A_EXP = A_TSB + 1
A_LN = A_EXP + 1
A_SQ1 = A_LN + 1
A_Y0 = A_SQ1
A_SQ2 = A_Y0 + B * L + 1
D_PREP = 11
D_ATTR = D_PREP + 1 + EDGE_BLOCKS
D_LOGIT = D_ATTR + 2
D_GIN0 = D_LOGIT + 3
D_LIN0 = D_GIN0 + 3
D_H1 = D_LIN0 + 3
D_GIN1 = D_H1 + 3
D_LIN1 = D_GIN1 + 3
D_SM = D_LIN1 + 4
D_SUM = D_SM + 1
D_VAR1 = D_SUM + 2 + 6
D_XS = D_VAR1 + 2 + 7 + 9
D_XT = D_XS + B * L // 4
D_Y0 = D_XT
D_VAR2 = D_Y0 + B * L + 2 + 2 + 3 + 6
D_OUT = D_VAR2 + 2

_INS = ['x', 'src', 'dst', 'edge_attr_16', 'edge_type_90', 'L0_gnn_eps1', 'L0_gnn_w1a', 'L0_gnn_b1a',
        'L0_gnn_w1b', 'L0_gnn_b1b', 'L0_gnn_eps2', 'L0_gnn_w2a', 'L0_gnn_b2a', 'L0_gnn_w2b',
        'L0_gnn_b2b', 'L1_gnn_Ws', 'L1_gnn_Wa', 'L1_gnn_weight', 'L1_gnn_w_comp']


def shape_constants():
    slots = np.zeros((KS, 3), np.float32)
    for s, part_of_w in enumerate((0, 1, 2, 0, 1, 0)):
        slots[s * F:(s + 1) * F, part_of_w] = 1
    return {
        "ident": np.eye(P, dtype=np.float32),
        "iota_hi": np.arange(HI).astype(np.float16),
        "lane_l": np.repeat(np.arange(L), F).astype(np.float16),
        "slots": slots,
    }


def kernel(**inputs):
    import concourse.bacc as _bacc
    from concourse.bass_utils import run_bass_kernel_spmd as _run

    nc = _bacc.Bacc("TRN2", target_bir_lowering=False, num_devices=1)
    arrays, args = {}, []
    for name in _INS:
        a = np.ascontiguousarray(inputs[name])
        if a.ndim == 0 or name.startswith("L0_gnn_eps"):
            a = a.reshape(1)
        arrays[f"in_{name}"] = a
        args.append(nc.dram_tensor(f"in_{name}", a.shape, mybir.dt.from_np(a.dtype), kind="ExternalInput").ap())
    for name, a in shape_constants().items():
        arrays[f"const_{name}"] = a
        args.append(nc.dram_tensor(f"const_{name}", a.shape, mybir.dt.from_np(a.dtype), kind="ExternalInput").ap())
    args.append(nc.dram_tensor("out_0", (NODES, F), FP32, kind="ExternalOutput").ap())
    build_gnn(nc, *args)
    r = _run(nc, [arrays], core_ids=[0])
    return r.results[0]["out_0"]
```

```python
import numpy as np
import concourse.bass as bass
import concourse.mybir as mybir
from contextlib import ExitStack

FP32 = mybir.dt.float32
BF16 = mybir.dt.bfloat16
FP16 = mybir.dt.float16
I32 = mybir.dt.int32
ALU = mybir.AluOpType
ACT = mybir.ActivationFunctionType
AX = mybir.AxisListType

P = 128
NODES, F = 3125, 16
EDGES = 103125
RELS, BASES = 90, 30
L = 8
B = 4
NODES_PAD = B * P * L
HI = -(-NODES // L)
FULL = NODES // (P * L)
LAST_P = (NODES - FULL * P * L) // L
LAST_L = NODES - FULL * P * L - LAST_P * L
TILES = -(-EDGES // P)
EDGE_BLOCKS = -(-TILES // P)
FULL_EB = TILES // P
LAST_T = EDGES // P - FULL_EB * P
LAST_E = EDGES - (FULL_EB * P + LAST_T) * P
CH = 13
CHUNKS = TILES // CH
assert CHUNKS * CH == TILES and CHUNKS % 2 == 0
PAD_DST = 8 * (HI + 100)
YW = F + 1
SLOTS = 6
KS = SLOTS * F
YCOLS = RELS * YW
YBANK = YCOLS // 3
EPS = 1e-5
NC = -(-NODES // P)
G = 2
W = 12
WINDOWS = TILES // G
CW = 13
WCHUNKS = WINDOWS // CW
assert WCHUNKS * CW * G == TILES and WCHUNKS % 2 == 1
SLOTS_W = 7
DSTS = NODES + W - 1
NB = -(-NODES // 512)
ROWS_P = [P] * FULL + [LAST_P + (LAST_L > 0)]


def node_rows(dram, sb):
    top = FULL * P * L
    mid = top + LAST_P * L
    yield dram[0:top, :].rearrange("(b p l) f -> p b (l f)", p=P, l=L), sb[:, 0:FULL, :]
    yield dram[top:mid, :].rearrange("(p l) f -> p (l f)", l=L), sb[0:LAST_P, FULL, :]
    yield (dram[mid:NODES, :].rearrange("(a l) f -> a (l f)", a=1),
           sb[LAST_P:LAST_P + 1, FULL, 0:LAST_L * F])


def edge_rows(dram, sb, w):
    top = FULL_EB * P * P
    mid = top + LAST_T * P
    yield dram[0:top, :].rearrange("(b t e) w -> t b (e w)", t=P, e=P), sb[:, 0:FULL_EB, :]
    yield dram[top:mid, :].rearrange("(t e) w -> t (e w)", e=P), sb[0:LAST_T, FULL_EB, :]
    yield (dram[mid:EDGES, :].rearrange("(a e) w -> a (e w)", a=1),
           sb[LAST_T:LAST_T + 1, FULL_EB, 0:LAST_E * w])


def build_gnn(nc, x, src, dst, attr, etype, eps1, w1a, b1a, w1b, b1b, eps2, w2a, b2a, w2b, b2b,
              ws, wa, weight, w_comp, ident_c, iota_hi_c, lane_l_c, slot_c, check_c, out):
    h_tab = nc.dram_tensor("h_tab", [NODES_PAD, F], FP32, kind="Internal").ap()
    t_tab = nc.dram_tensor("t_tab", [F * RELS, F], FP32, kind="Internal").ap()
    y_tab = nc.dram_tensor("y_tab", [sum(ROWS_P) * L * RELS, YW], FP32, kind="Internal").ap()

    ctx = ExitStack()
    with ctx:
        def sb(name, shape, dt=FP32):
            return ctx.enter_context(nc.sbuf_tensor(name, shape, dt))

        def sem(name):
            return ctx.enter_context(nc.semaphore(name))

        arena = sb("arena", [P, NC * DSTS], BF16)
        counts = arena[:, :].rearrange("p (c d) -> p c d", c=NC)
        cursor = [0]

        def carve(shape, dt=FP32):
            two = 2 if dt in (FP32, I32) else 1
            n = int(np.prod(shape[1:])) * two
            at = cursor[0]
            cursor[0] += -(-n // 16) * 16
            assert cursor[0] <= NC * DSTS, cursor[0]
            a = arena[0:shape[0], at:at + n]
            return a if dt == BF16 else a.bitcast(dt)

        ident = sb("ident", [P, P])
        ident_bf = sb("ident_bf", [P, P], BF16)
        iota_hi = sb("iota_hi", [P, HI], FP16)
        iota_l = sb("iota_l", [P, L * F], FP16)
        slot_mask = sb("slot_mask", [KS, 3])
        zeros = sb("zeros", [P, HI + 1], BF16)
        kron = sb("kron", [P, 4, P])
        bias = sb("bias", [P, 4, F])
        eps = sb("eps", [P, 2])
        ws_sb = sb("ws_sb", [F, F])
        ws_rep = sb("ws_rep", [F, SLOTS, F])
        wa_sb = sb("wa_sb", [F, 3])
        wa_rep = sb("wa_rep", [F, 2, P])
        u_rows = sb("u_rows", [P, 2, F])
        u_src = sb("u_src", [KS, 1])
        w_stack = sb("w_stack", [KS, YCOLS], BF16)
        row_idx = sb("row_idx", [P, EDGE_COLS], I32)
        dst_hl = sb("dst_hl", [P, 2, EDGE_COLS], FP16)
        logit_raw = sb("logit_raw", [P, EDGE_COLS])
        attr_ring = sb("attr_ring", [P, 2, ATTR_E * F])
        key = sb("key", [P, 2, TILES], FP16)
        key_prev = sb("key_prev", [P, WINDOWS], FP16)
        first = sb("first", [1, WCHUNKS, 16], I32)
        key_st = sb("key_st", [P, 2, 2, CW * G])
        prev_st = sb("prev_st", [P, 2, CW])
        n_lo, n_key, n_prev = SLOTS_W * G * P, SLOTS_W * G * W * NC, 2 * CW * (NC + 1)
        window = sb("window", [P, n_lo + n_key + n_prev], BF16)
        win_lo = window[:, 0:n_lo].rearrange("p (s g k) -> p s g k", s=SLOTS_W, g=G)
        win_key = window[:, n_lo:n_lo + n_key].rearrange("p (s g k) -> p s g k", s=SLOTS_W, g=G)
        win_prev = window[:, n_lo + n_key:].rearrange("p (k w c) -> p k w c", k=2, w=CW)
        flag_f = sb("flag_f", [1, 8])
        flag_i = sb("flag_i", [1, 1], I32)
        sum_t = window[:, :].bitcast(FP32)
        x_c = sb("x_c", [P, NC, F])
        x_parts = sb("x_parts", [P, NC, 3, F], BF16)
        idx_st = sb("idx_st", [P, 2, CH], I32)
        meta_st = sb("meta_st", [P, 2, 3, CH])
        xn = sb("xn", [P, B, L * F])
        hn = sb("hn", [P, B, L * F])
        x2n = hn
        t1 = sb("t1", [P, B, L * F])
        t2 = sb("t2", [P, B, L * F])
        agg_n = t1
        hT = t2
        st1 = sb("st1", [P, B * L])
        st2 = sb("st2", [P, B * L])

        src_idx = carve([P, EDGE_COLS], I32)
        base = cursor[0]
        ints = carve([P, 5 * EDGE_COLS], I32).rearrange("p (k b e) -> p k b e", k=5, e=P)
        src_i, dst_i, type_i, hi_i, lo_i = (ints[:, k] for k in range(5))
        raw = carve([P, 4 * EDGE_COLS]).rearrange("p (k n) -> p k n", k=4)
        SRC, ROW, DHI, DLO = range(4)
        dst_t = carve([P, EDGE_COLS])
        firsts = carve([P, TILES])
        int_a = carve([P, TILES], I32)
        src_hi = carve([P, TILES])
        tmp = carve([P, TILES])
        tmp2 = carve([P, TILES])
        check = carve([P, 3 * P]).rearrange("p (k m) -> p k m", k=3)
        comp_sb = carve([RELS, BASES])
        compT = carve([BASES, RELS])
        v_sb = carve([BASES, F * F]).rearrange("b (i o) -> b i o", i=F)
        t_sb = carve([RELS, F * F]).rearrange("r (i o) -> r i o", i=F)
        w_full = carve([KS, RELS * F]).rearrange("k (r f) -> k r f", r=RELS)
        w_ext = carve([KS, YCOLS])
        w_hi, w_mid, w_lo = (carve([KS, YCOLS], BF16) for _ in range(3))
        cursor[0] = base
        rows = carve([P, 2 * CH * YW]).rearrange("p (k c w) -> p k c w", k=2, c=CH)
        msg = carve([P, CH * 2 * F]).rearrange("p (c f) -> p c f", c=CH)
        rest = carve([P, CH * 2 * F]).rearrange("p (c f) -> p c f", c=CH)
        part = [carve([P, CH * 2 * F], BF16).rearrange("p (c f) -> p c f", c=CH) for _ in range(3)]
        scale = carve([P, CH])
        logit = carve([P, EDGE_COLS])
        oh_hi = carve([P, 2 * CH * (HI + 1)], BF16).rearrange("p (k c h) -> p k c h", k=2, c=CH)
        oh_l = carve([P, CH * P], BF16).rearrange("p (c m) -> p c m", c=CH)
        agg_sb = carve([P, 2 * B * P]).rearrange("p (h n) -> p h n", h=2)
        xs = carve([P, B * L * KS], BF16).rearrange("p (c s f) -> p c s f", c=B * L, s=SLOTS)
        xsT = carve([KS, B * L * P], BF16).rearrange("p (c n) -> p c n", c=B * L)
        end = cursor[0]
        spread = carve([P, 2 * CH * 6 * P], BF16).rearrange("p (k c q m) -> p k c q m", k=2, c=CH, q=6)
        cursor[0] = end
        y_sb = carve([P, 3 * YCOLS]).rearrange("p (k w) -> p k w", k=3)

        PS = [ctx.enter_context(nc.psum_tensor(f"ps{k}", [P, 512], FP32)) for k in range(8)]

        s_const = sem("const_loaded")
        s_w = sem("weights_loaded")
        s_kron = sem("kron_loaded")
        s_x = sem("x_loaded")
        s_xc = sem("x_chunks_loaded")
        s_e = sem("edges_loaded")
        s_attr = [sem(f"attr_loaded{k}") for k in range(2)]
        s_attr_used = sem("attr_used")
        s_attr_sum = sem("attr_sum_step")
        s_pads = sem("pads_filled")
        s_dve = sem("dve_step")
        s_zero = sem("zeros_written")
        s_prep = sem("edges_split")
        s_tr = sem("edges_transposed")
        s_tc = sem("edges_copied")
        s_u = sem("logit_vectors")
        s_uc = sem("logit_vectors_copied")
        s_t = sem("t_product")
        s_tsb = sem("t_copied")
        s_t_out = sem("t_written")
        s_w_in = sem("w_rel_loaded")
        s_dt = sem("dst_joined")
        s_first = sem("firsts_and_diffs")
        s_dmin = sem("diff_min")
        s_dminT = sem("diff_min_transposed")
        s_flag = sem("flag_written")
        s_tab = sem("h_written")
        s_aggn = sem("agg_in_node_layout")
        s_in = sem("linear_input")
        s_inT = sem("linear_input_transposed")
        s_hT = sem("linear_input_copied")
        s_lin = sem("linear_product")
        s_h1 = sem("hidden_written")
        s_sm = sem("shifted_logits")
        s_exp = sem("exp_done")
        s_sum = sem("exp_sum")
        s_ln = sem("ln_done")
        s_var = sem("variance")
        s_sqrt = sem("sqrt_done")
        s_lT = sem("edge_logits_transposed")
        s_xs = sem("x2_parts")
        s_xT = sem("x2_parts_transposed")
        s_xTc = sem("x2_parts_copied")
        s_y = sem("y_product")
        s_ya = sem("y_copied_by_act")
        s_yv = sem("y_copied_by_dve")
        s_y_out = [sem(f"y_written{k}") for k in range(3)]
        s_logit = sem("edge_logits_copied")
        s_res = sem("result")
        s_out = sem("out_written")
        s_begun = sem("gathers_begun")
        R = range(3)
        s_idx = [sem(f"idx_staged{r}") for r in R]
        s_meta = [sem(f"meta_staged{r}") for r in R]
        s_rows = [[sem(f"rows_landed{r}_{k}") for k in range(2)] for r in R]
        s_split = [sem(f"split_step{r}") for r in R]
        s_ready = [sem(f"operands_ready{r}") for r in R]
        s_used = [sem(f"operands_used{r}") for r in R]
        s_agg = [sem(f"agg_done{r}") for r in R]
        s_aggc = [sem(f"agg_copied{r}") for r in R]
        s_aggT = [sem(f"agg_transposed{r}") for r in R]
        s_keys = sem("keys_staged")
        s_prev = sem("prev_keys_ready")
        s_oh = sem("window_operands_ready")
        s_win = sem("window_product")
        s_cop = sem("window_copied")
        s_xp = sem("x_parts_ready")
        s_den = sem("dense_product")
        s_dca = sem("dense_copied_by_act")
        s_dcv = sem("dense_copied_by_dve")
        s_denT = sem("dense_transposed")

        block = ctx.enter_context(nc.Block())

        def sorted_flag(eng):
            eng.wait_ge(s_flag, 1)
            return eng.value_load(flag_i[0:1, 0:1], min_val=0, max_val=1)

        def freed(n, j):
            if j >= SLOTS_W:
                return n * CW + j - SLOTS_W
            if isinstance(n, int) and n == 0:
                return None
            return (n - 1) * CW + (j + SLOTS_W if j + SLOTS_W < CW else j)

        @block.sync
        def _(sp):
            sp.wait_ge(s_pads, 4)
            for a, t in ((src, src_i), (dst, dst_i), (etype, type_i)):
                for d, s in edge_rows(a.rearrange("(e w) -> e w", w=1), t, 1):
                    sp.dma_start(s, d).then_inc(s_e, 16)
            sp.dma_start(ident[:, :], ident_c).then_inc(s_const, 16)
            sp.dma_start(iota_hi[:, :], iota_hi_c.partition_broadcast(P)).then_inc(s_const, 16)
            sp.dma_start(iota_l[:, :], lane_l_c.partition_broadcast(P)).then_inc(s_const, 16)
            sp.dma_start(slot_mask[:, :], slot_c).then_inc(s_const, 16)
            sp.dma_start(check, check_c.rearrange("p k m -> p k m")).then_inc(s_const, 16)
            for d, s in node_rows(x, xn):
                sp.dma_start(s, d).then_inc(s_x, 16)
            sp.wait_ge(s_pads, 6)
            top = (NC - 1) * P
            sp.dma_start(x_c[:, 0:NC - 1, :], x[0:top, :].rearrange("(c p) f -> p c f", p=P)).then_inc(s_xc, 16)
            sp.dma_start(x_c[0:NODES - top, NC - 1, :], x[top:NODES, :]).then_inc(s_xc, 16)
            sp.wait_ge(s_tsb, 1)
            sp.dma_start(t_tab.rearrange("(i r) o -> r i o", r=RELS), t_sb).then_inc(s_t_out, 16)
            sp.wait_ge(s_t_out, 16)
            for k in range(SLOTS):
                sp.dma_start(w_full[k * F:(k + 1) * F], t_tab.rearrange("(r i) o -> i r o", i=F)).then_inc(s_w_in, 16)
            for n in range(ATTR_N):
                b, q = divmod(n, P // ATTR_E)
                if n >= 2:
                    sp.wait_ge(s_attr_used, n - 1)
                for d, s in attr_rows(attr, attr_ring[:, n % 2, :], b, q):
                    sp.dma_start(s, d).then_inc(s_attr[n % 2], 16)
            even = sorted_flag(sp)
            sp.wait_ge(s_h1, 1)
            sp.dma_start(h_tab.rearrange("(b p l) f -> p b (l f)", p=P, l=L), hn[:, :, :]).then_inc(s_tab, 16)
            with sp.If(even > 0):
                sp.wait_ge(s_tab, 16)
                sp.wait_ge(s_xp, 4)
                sp.dma_start(x_c[:, :, :], h_tab[0:NC * P, :].rearrange("(c p) f -> p c f", p=P)).then_inc(s_xc, 16)
            sp.end_ifs()
            yv = y_tab.rearrange("(p l r) w -> l p (r w)", l=L, r=RELS)
            for c in range(B * L):
                n = ROWS_P[c // L]
                sp.wait_ge(s_ya, c + 1)
                sp.wait_ge(s_yv, c + 1)
                sp.dma_start(yv[c % L, (c // L) * P:(c // L) * P + n], y_sb[0:n, c % 3, :]).then_inc(s_y_out[c % 3], 16)
            sp.wait_ge(s_res, 1)
            for d, s in node_rows(out, t1):
                sp.dma_start(d, s).then_inc(s_out, 16)
            sp.wait_ge(s_out, 48)

        @block.gpsimd
        def _(pool):
            pool.wait_ge(s_uc, 1)
            for n in range(ATTR_N):
                landed = sum(16 * len(list(attr_rows(attr, attr_ring[:, 0, :], *divmod(m, P // ATTR_E))))
                             for m in range(n % 2, n + 1, 2))
                pool.wait_ge(s_attr[n % 2], landed)
                a3 = attr_ring[:, n % 2, :].rearrange("p (e f) -> p e f", f=F)
                pool.tensor_tensor(a3, a3, u_rows[:, 0:1, :].broadcast_to([P, ATTR_E, F]),
                                   ALU.mult).then_inc(s_attr_sum, 1)
                at, w = 4 * n + 1, F // 2
                while w > 1:
                    pool.wait_ge(s_attr_sum, at)
                    pool.tensor_tensor(a3[:, :, 0:w], a3[:, :, 0:w], a3[:, :, w:2 * w], ALU.add).then_inc(s_attr_sum, 1)
                    at, w = at + 1, w // 2
                pool.wait_ge(s_attr_sum, at)
                pool.tensor_tensor(logit_raw[:, n * ATTR_E:(n + 1) * ATTR_E], a3[:, :, 0], a3[:, :, 1],
                                   ALU.add).then_inc(s_attr_used, 1)

            def gather(r, n, k, table, width):
                pool.wait_ge(s_idx[r], n + 1)
                if not isinstance(n, int) or n >= 2:
                    pool.wait_ge(s_ready[r], n - 1)
                pool.sem_inc(s_begun, 1)
                for j in range(CH):
                    pool.indirect_dma_start(
                        rows[:, k, j, 0:width], None, table,
                        bass.IndirectOffsetOnAxis(ap=idx_st[:, k, j:j + 1], axis=0),
                    ).then_inc(s_rows[r][k], 16)

            def gathers(r, table, width):
                gather(r, 0, 0, table, width)
                gather(r, 1, 1, table, width)
                with pool.Fori(2, CHUNKS, 2) as n:
                    gather(r, n, 0, table, width)
                    gather(r, n + 1, 1, table, width)

            even = sorted_flag(pool)
            with pool.If(even < 1):
                gathers(0, x, F)
                pool.wait_ge(s_tab, 16)
                gathers(1, h_tab, F)
            pool.end_ifs()
            for k in range(3):
                pool.wait_ge(s_y_out[k], 16 * len(range(k, B * L, 3)))
            gathers(2, y_tab, YW)

        @block.scalar
        def _(act):
            act.wait_ge(s_pads, 5)
            act.dma_start(ws_sb[:, :], ws).then_inc(s_w, 16)
            act.dma_start(wa_sb[:, :], wa.rearrange("a (k o) -> (a o) k", k=3),
                          allow_slow_non_contiguous=True).then_inc(s_w, 16)
            act.dma_start(comp_sb, w_comp).then_inc(s_w, 16)
            act.dma_start(v_sb, weight.rearrange("b i o -> (b i o)").rearrange(
                "(i b o) -> b i o", i=F, b=BASES)).then_inc(s_w, 16)
            for k, a in enumerate((eps1, eps2)):
                act.dma_start(eps[:, k:k + 1], a.partition_broadcast(P)).then_inc(s_w, 16)
            for k, a in enumerate((b1a, b1b, b2a, b2b)):
                act.dma_start(bias[:, k, :], a.partition_broadcast(P)).then_inc(s_w, 16)

            into = {SRC: src_idx, ROW: row_idx[:, :], DHI: dst_hl[:, 0, :], DLO: dst_hl[:, 1, :]}
            for g, (k, at, width) in enumerate(EDGE_T):
                act.wait_ge(s_tr, g + 1)
                nc.scalar.copy(into[k][:, at:at + width], PS[g % 2][:, 0:width]).then_inc(s_tc, 1)
            act.wait_ge(s_u, 1)
            nc.scalar.copy(u_rows[:, :, :], PS[2][:, 0:2 * F].rearrange("p (k f) -> p k f", k=2)).then_inc(s_uc, 1)
            nc.scalar.copy(u_src[:, :], PS[2][0:KS, 64:65]).then_inc(s_uc, 1)
            nc.scalar.copy(compT, PS[3][0:BASES, 0:RELS]).then_inc(s_uc, 1)
            act.wait_ge(s_t, 1)
            nc.scalar.copy(t_sb, PS[3][0:RELS, 128:128 + F * F].rearrange("r (i o) -> r i o", i=F)).then_inc(s_tsb, 1)
            for k, a in enumerate((w1a, w1b, w2a, w2b)):
                for l in range(L):
                    act.dma_start(kron[l * F:(l + 1) * F, k, l * F:(l + 1) * F], a).then_inc(s_kron, 16)

            def stage(r, n, k, which):
                if not isinstance(n, int) or n >= 2:
                    act.wait_ge(s_rows[r][k], 8 * CH * (n - k))
                act.copy(idx_st[:, k, :], which[:, bass.ds(n * CH, CH)]).then_inc(s_idx[r], 1)
                if not isinstance(n, int) or n >= 2:
                    act.wait_ge(s_ready[r], n - 1)
                act.copy(meta_st[:, k, 0:2, :], dst_hl[:, :, bass.ds(n * CH, CH)]).then_inc(s_meta[r], 1)
                if r == 2:
                    act.copy(meta_st[:, k, 2, :], logit[:, bass.ds(n * CH, CH)]).then_inc(s_meta[r], 1)

            def stages(r, which):
                stage(r, 0, 0, which)
                stage(r, 1, 1, which)
                with act.Fori(2, CHUNKS, 2) as n:
                    stage(r, n, 0, which)
                    stage(r, n + 1, 1, which)

            def stage_keys(n, k):
                if not isinstance(n, int) or n >= 2:
                    act.wait_ge(s_oh, (n - 1) * CW)
                act.copy(key_st[:, k, :, :], key[:, :, bass.ds(n * CW * G, CW * G)]).then_inc(s_keys, 1)
                act.copy(prev_st[:, k, :], key_prev[:, bass.ds(n * CW, CW)]).then_inc(s_keys, 1)

            def windows(n, k):
                _, at = nc.values_load_multi_w_load_instructions(
                    first[0:1, bass.ds(n, 1), 0:CW].rearrange("a n w -> a (n w)"),
                    engines=(mybir.EngineType.Activation,), min_val=0, max_val=NODES - 1,
                    skip_runtime_bounds_check_because="the flag is up only for node numbers")
                for j in range(CW):
                    act.wait_ge(s_win, n * CW + j + 1)
                    if not isinstance(n, int) or n * CW + j >= 1:
                        act.wait_ge(s_cop, n * CW + j)
                    nc.scalar.copy(counts[:, :, bass.ds(at[j], W)],
                                   PS[j % SLOTS_W][:, 0:W * NC].rearrange("p (d c) -> p c d", c=NC)).then_inc(s_cop, 1)
                    if j == CW // 2:
                        if not isinstance(n, int) or n + 2 < WCHUNKS:
                            stage_keys(n + 2, k)

            def dense_copy(r):
                for q in range(0, NB, 2):
                    act.wait_ge(s_den, (r * NB) + q + 1)
                    n = min(512, NODES - q * 512)
                    nc.scalar.copy(sum_t[0:3 * F, q * 512:q * 512 + n], PS[q][0:3 * F, 0:n]).then_inc(s_dca, 1)

            even = sorted_flag(act)
            with act.If(even > 0):
                act.wait_ge(s_tc, len(EDGE_T))
                stage_keys(0, 0)
                stage_keys(1, 1)
                windows(0, 0)
                with act.Fori(1, WCHUNKS - 3, 2) as n:
                    windows(n, 1)
                    windows(n + 1, 0)
                windows(WCHUNKS - 2, 1)
                windows(WCHUNKS - 1, 0)
                dense_copy(0)
                dense_copy(1)
            with act.Else():
                stages(0, src_idx)
                act.wait_ge(s_ready[0], CHUNKS)
                stages(1, src_idx)
                act.wait_ge(s_ready[1], CHUNKS)
            act.wait_ge(s_sm, 1)
            nc.scalar.activation(t2[:, :, :], t1[:, :, :], ACT.Exp).then_inc(s_exp, 1)
            act.wait_ge(s_sum, 1)
            nc.scalar.activation(st2[:, :], st1[:, :], ACT.Ln).then_inc(s_ln, 1)
            act.wait_ge(s_var, 1)
            nc.scalar.activation(st2[:, :], st1[:, :], ACT.Sqrt).then_inc(s_sqrt, 1)
            for c in range(B * L):
                m = ROWS_P[c // L]
                act.wait_ge(s_y, c + 1)
                if c >= 3:
                    act.wait_ge(s_y_out[c % 3], 16 * (c // 3))
                s = 2 + 3 * (c % 2)
                if c % 2 == 0:
                    nc.scalar.copy(y_sb[0:m, c % 3, YBANK:2 * YBANK], PS[s + 1][0:m, 0:YBANK])
                nc.scalar.copy(y_sb[0:m, c % 3, 0:YBANK], PS[s][0:m, 0:YBANK]).then_inc(s_ya, 1)
            act.wait_ge(s_logit, 2)
            stages(2, row_idx)
            act.wait_ge(s_var, 2)
            nc.scalar.activation(st2[:, :], st1[:, :], ACT.Sqrt).then_inc(s_sqrt, 1)

        @block.vector
        def _(dve):
            count = [0]
            v = nc.vector

            def chain(ins):
                count[0] += 1
                ins.then_inc(s_dve, 1)
                dve.wait_ge(s_dve, count[0])

            v.memset(dst_i[:, FULL_EB, :], PAD_DST).then_inc(s_pads, 1)
            v.memset(src_i[:, FULL_EB, :], 0).then_inc(s_pads, 1)
            v.memset(type_i[:, FULL_EB, :], 0).then_inc(s_pads, 1)
            v.memset(xn[:, FULL:, :], 0.0).then_inc(s_pads, 1)
            v.memset(kron[:, :, :], 0.0).then_inc(s_pads, 1)
            v.memset(x_c[:, NC - 1, :], 0.0).then_inc(s_pads, 1)
            v.memset(agg_n[:, FULL, :], 0.0)
            v.memset(key_prev[:, 0:1], NO_KEY)
            v.memset(zeros[:, :], 0.0).then_inc(s_zero, 1)
            dve.wait_ge(s_w, 16 * 10)
            chain(v.tensor_scalar(eps[:, :], eps[:, :], 1.0, None, ALU.add))
            v.tensor_copy(ws_rep[:, :, :], ws_sb[:, :].rearrange("o (a i) -> o a i", a=1)
                          .broadcast_to([F, SLOTS, F]))
            v.tensor_copy(wa_rep[:, :, :], wa_sb[:, 1:3].rearrange("o (k a) -> o k a", a=1)
                          .broadcast_to([F, 2, P]))
            dve.wait_ge(s_e, 16 * 9)
            raw3 = [raw[:, k, :].rearrange("p (b e) -> p b e", b=EDGE_BLOCKS) for k in range(4)]
            v.tensor_scalar(hi_i, dst_i, 3, None, ALU.arith_shift_right)
            v.tensor_scalar(lo_i, dst_i, L - 1, None, ALU.bitwise_and)
            chain(v.tensor_copy(raw3[SRC], src_i))
            v.tensor_copy(raw3[DHI], hi_i)
            v.tensor_copy(raw3[DLO], lo_i)
            chain(v.tensor_scalar(raw3[ROW], raw3[SRC], float(RELS), None, ALU.mult))
            v.tensor_tensor(raw3[ROW], raw3[ROW], type_i, ALU.add)
            dve.wait_ge(s_const, 16 * 5)
            v.tensor_copy(ident_bf[:, :], ident[:, :]).then_inc(s_prep, 1)

            dve.wait_ge(s_tc, len(EDGE_T))
            v.scalar_tensor_tensor(out=dst_t, in0=dst_hl[:, 0, :], scalar=float(L), in1=dst_hl[:, 1, :],
                                   op0=ALU.mult, op1=ALU.add).then_inc(s_dt, 1)
            chain(v.tensor_scalar(int_a, src_idx[:, 0:TILES], P - 1, None, ALU.bitwise_and))
            chain(v.tensor_copy(key[:, 0, :], int_a))
            chain(v.tensor_scalar(int_a, src_idx[:, 0:TILES], 7, None, ALU.arith_shift_right))
            chain(v.tensor_copy(src_hi, int_a))
            dve.wait_ge(s_first, 1)
            v.tensor_copy(firsts[:, 0:512], PS[4][:, :])
            v.tensor_copy(firsts[:, 512:TILES], PS[5][:, 0:TILES - 512])
            v.tensor_reduce(tmp2[:, 0:1], PS[6][:, :], AX.X, ALU.min)
            chain(v.tensor_reduce(tmp2[:, 1:2], PS[7][:, 0:TILES - 512], AX.X, ALU.min))
            v.tensor_reduce(tmp2[:, 2:3], tmp2[:, 0:2], AX.X, ALU.min).then_inc(s_dmin, 1)
            w1 = lambda t: t.rearrange("p (g q) -> p g q", q=G)
            chain(v.tensor_tensor(w1(tmp), w1(dst_t[:, 0:TILES]),
                                  w1(firsts)[:, :, 0:1].broadcast_to([P, WINDOWS, G]), ALU.subtract))
            chain(v.tensor_scalar(tmp, tmp, float(NO_KEY // NC), float(NC), ALU.min, ALU.mult))
            chain(v.tensor_tensor(key[:, 1, :], tmp, src_hi, ALU.add))
            gp = WINDOWS - 1
            before = lambda t: w1(t)[:, 0:gp, G - 1]
            chain(v.tensor_tensor(tmp[:, 0:gp], before(dst_t[:, 0:TILES]), w1(firsts)[:, 1:, 0], ALU.is_equal))
            chain(v.tensor_scalar(tmp[:, 0:gp], tmp[:, 0:gp], -float(NO_KEY), float(NO_KEY), ALU.mult, ALU.add))
            chain(v.tensor_tensor(key_prev[:, 1:], tmp[:, 0:gp], before(src_hi), ALU.add))
            chain(v.tensor_copy(first[0:1, :, 0:CW], firsts[0:1, 0:TILES].rearrange(
                "a (n w q) -> a n w q", w=CW, q=G)[:, :, :, 0]))
            f1 = firsts[0:1, :]
            chain(v.tensor_tensor(tmp[0:1, 0:TILES - 1], f1[:, 1:], f1[:, 0:TILES - 1], ALU.subtract))
            chain(v.tensor_reduce(flag_f[:, 0:1], tmp[0:1, 0:TILES - 1], AX.X, ALU.min))
            fw = w1(f1)[:, :, 0]
            chain(v.tensor_tensor(tmp[0:1, 0:gp], fw[:, 1:], fw[:, 0:gp], ALU.subtract))
            v.tensor_scalar(tmp[0:1, gp:gp + 1], fw[:, gp:gp + 1], -1.0, float(NODES), ALU.mult, ALU.add)
            chain(v.tensor_scalar(flag_f[:, 1:2], fw[:, 0:1], 0.0, None, ALU.is_equal))
            chain(v.tensor_reduce(flag_f[:, 2:3], tmp[0:1, 0:WINDOWS], AX.X, ALU.max))
            dve.wait_ge(s_dminT, 1)
            chain(v.tensor_reduce(flag_f[:, 3:4], PS[2][0:1, 128:256], AX.X, ALU.min))
            v.tensor_scalar(flag_f[:, 4:5], flag_f[:, 0:1], 1.0, None, ALU.is_ge)
            v.tensor_scalar(flag_f[:, 5:6], flag_f[:, 2:3], float(W - 1), None, ALU.is_le)
            chain(v.tensor_scalar(flag_f[:, 6:7], flag_f[:, 3:4], 0.0, None, ALU.is_ge))
            chain(v.tensor_tensor(flag_f[:, 4:5], flag_f[:, 4:5], flag_f[:, 5:6], ALU.mult))
            chain(v.tensor_tensor(flag_f[:, 6:7], flag_f[:, 6:7], flag_f[:, 1:2], ALU.mult))
            chain(v.tensor_tensor(flag_f[:, 4:5], flag_f[:, 4:5], flag_f[:, 6:7], ALU.mult))
            dve.wait_ge(s_w_in, 16 * SLOTS)
            dve.wait_ge(s_uc, 3)
            we3 = w_ext.rearrange("k (r w) -> k r w", w=YW)
            v.tensor_copy(we3[:, :, 0:F], w_full)
            chain(v.tensor_copy(we3[:, :, F:YW], u_src[:, :].rearrange("p (a b) -> p a b", a=1)
                                .broadcast_to([KS, RELS, 1])))
            chain(v.tensor_copy(w_hi, w_ext))
            chain(v.tensor_tensor(w_ext, w_ext, w_hi, ALU.subtract))
            chain(v.tensor_copy(w_mid, w_ext))
            chain(v.tensor_tensor(w_lo, w_ext, w_mid, ALU.subtract))
            chain(v.tensor_scalar(w_stack[:, :], w_hi, slot_mask[:, 0:1], None, ALU.mult))
            chain(v.scalar_tensor_tensor(out=w_stack[:, :], in0=w_mid, scalar=slot_mask[:, 1:2],
                                         in1=w_stack[:, :], op0=ALU.mult, op1=ALU.add))
            chain(v.scalar_tensor_tensor(out=w_stack[:, :], in0=w_lo, scalar=slot_mask[:, 2:3],
                                         in1=w_stack[:, :], op0=ALU.mult, op1=ALU.add))
            v.tensor_copy(flag_i[:, :], flag_f[:, 4:5]).then_inc(s_flag, 1)

            def window_chunk(n, k):
                dve.wait_ge(s_keys, 2 * n + 2)
                if not isinstance(n, int) or n >= 2:
                    dve.wait_ge(s_win, (n - 1) * CW)
                v.tensor_tensor(win_prev[:, k, :, 0:NC], iota_hi[:, 0:NC].rearrange("p (a c) -> p a c", a=1)
                                .broadcast_to([P, CW, NC]),
                                prev_st[:, k, :].rearrange("p (w a) -> p w a", a=1).broadcast_to([P, CW, NC]),
                                ALU.is_equal).then_inc(s_prev, 1)
                for j in range(CW):
                    s, used = j % SLOTS_W, freed(n, j)
                    if used is not None:
                        dve.wait_ge(s_win, used + 2)
                    for q in range(G):
                        v.tensor_scalar(win_lo[:, s, q, :], iota_hi[:, 0:P], key_st[:, k, 0, G * j + q:G * j + q + 1],
                                        None, ALU.is_equal)
                    for q in range(G):
                        last = v.tensor_scalar(win_key[:, s, q, :], iota_hi[:, 0:W * NC],
                                               key_st[:, k, 1, G * j + q:G * j + q + 1], None, ALU.is_equal)
                    last.then_inc(s_oh, 1)

            def dense(r):
                xp = [x_parts[:, :, q, :] for q in range(3)]
                dve.wait_ge(s_xc, 32 + 16 * r)
                v.tensor_copy(xp[0], x_c[:, :, :]).then_inc(s_xp, 1)
                dve.wait_ge(s_xp, 4 * r + 1)
                v.tensor_tensor(x_c[:, :, :], x_c[:, :, :], xp[0], ALU.subtract).then_inc(s_xp, 1)
                dve.wait_ge(s_xp, 4 * r + 2)
                v.tensor_copy(xp[1], x_c[:, :, :]).then_inc(s_xp, 1)
                dve.wait_ge(s_xp, 4 * r + 3)
                v.tensor_tensor(xp[2], x_c[:, :, :], xp[1], ALU.subtract).then_inc(s_xp, 1)
                if r == 0:
                    dve.wait_ge(s_win, WINDOWS)
                    v.memset(sum_t[0:3 * F, NODES:NODES + W], 0.0)
                for q in range(1, NB, 2):
                    dve.wait_ge(s_den, r * NB + q + 1)
                    n = min(512, NODES - q * 512)
                    v.tensor_copy(sum_t[0:3 * F, q * 512:q * 512 + n], PS[q][0:3 * F, 0:n]).then_inc(s_dcv, 1)
                dve.wait_ge(s_denT, r + 1)
                for b in range(B):
                    m = ROWS_P[b]
                    last = v.tensor_reduce(agg_n[0:m, b, :].rearrange("p (l f) -> p l f", f=F),
                                           PS[b][0:m, 0:L * 3 * F].rearrange("p (l s f) -> p l f s", s=3, f=F),
                                           AX.X, ALU.add)
                chain_in(last)

            def edge_chunk(r, n, k):
                w = F if r < 2 else 2 * F
                steps = 4 if r < 2 else 6
                got = rows[:, k, :, :]

                def split(ins, i):
                    ins.then_inc(s_split[r], 1)
                    return n * steps + i + 1

                dve.wait_ge(s_meta[r], (n + 1) * (2 if r == 2 else 1))
                if not isinstance(n, int) or n >= 2:
                    dve.wait_ge(s_used[r], n - 1)
                for j in range(CH):
                    v.tensor_scalar(oh_hi[:, k, j, 0:HI], iota_hi[:, :], meta_st[:, k, 0, j:j + 1],
                                    None, ALU.is_equal)
                if not isinstance(n, int) or n >= 1:
                    dve.wait_ge(s_ready[r], n)
                for j in range(CH):
                    v.tensor_scalar(oh_l[:, j, :], iota_l[:, :], meta_st[:, k, 1, j:j + 1],
                                    None, ALU.is_equal)
                dve.wait_ge(s_rows[r][k], 8 * CH * (n - k + 2))
                i = 0
                val = got[:, :, 0:F]
                if r == 2:
                    at = split(v.tensor_tensor(scale, got[:, :, F], meta_st[:, k, 2, :], ALU.add), 0)
                    dve.wait_ge(s_split[r], at)
                    v.tensor_tensor(msg[:, :, 0:F], val, scale.rearrange("p (c a) -> p c a", a=1)
                                    .broadcast_to([P, CH, F]), ALU.mult)
                    at = split(v.tensor_copy(msg[:, :, F:2 * F], val), 1)
                    dve.wait_ge(s_split[r], at)
                    val, i = msg, 2
                p0, p1, p2 = (q[:, :, 0:w] for q in part)
                rs = rest[:, :, 0:w]
                dve.wait_ge(s_split[r], split(v.tensor_copy(p0, val), i))
                dve.wait_ge(s_split[r], split(v.tensor_tensor(rs, val, p0, ALU.subtract), i + 1))
                dve.wait_ge(s_split[r], split(v.tensor_copy(p1, rs), i + 2))
                dve.wait_ge(s_split[r], split(v.tensor_tensor(p2, rs, p1, ALU.subtract), i + 3))
                oh4 = oh_l.rearrange("p c (l f) -> p c l f", f=F)
                for h in range(w // F):
                    for q in range(3):
                        o = spread[:, k, :, 3 * h + q, :].rearrange("p c (l f) -> p c l f", f=F)
                        s = part[q][:, :, h * F:(h + 1) * F].rearrange("p c (a f) -> p c a f", a=1)
                        last = v.tensor_tensor(o, oh4, s.broadcast_to([P, CH, L, F]), ALU.mult)
                last.then_inc(s_ready[r], 1)

            def edges(r, halves):
                v.memset(agg_sb[:, :, HI:], 0.0)
                edge_chunk(r, 0, 0)
                edge_chunk(r, 1, 1)
                with dve.Fori(2, CHUNKS, 2) as n:
                    edge_chunk(r, n, 0)
                    edge_chunk(r, n + 1, 1)
                dve.wait_ge(s_agg[r], 1)
                for h in range(halves):
                    last = v.tensor_copy(agg_sb[:, h, 0:HI], PS[h][:, 0:HI])
                last.then_inc(s_aggc[r], 1)
                dve.wait_ge(s_aggT[r], 1)

            flat = lambda t: t[:, :, :].rearrange("p b (l f) -> p (b l) f", f=F)
            row = lambda s: s[:, :].rearrange("p (c a) -> p c a", a=1).broadcast_to([P, B * L, F])
            brow = lambda k: bias[:, k:k + 1, :].broadcast_to([P, B * L, F])
            n_in = [0]

            def chain_in(ins):
                ins.then_inc(s_aggn, 1)

            def linear(k):
                n_in[0] += 1
                dve.wait_ge(s_inT, n_in[0])
                v.tensor_copy(hT[:, :, :], PS[4][:, :].rearrange("p (b n) -> p b n", b=B)).then_inc(s_hT, 1)
                dve.wait_ge(s_lin, n_in[0])
                chain(v.tensor_tensor(flat(t1), PS[3][:, :].rearrange("p (c f) -> p c f", f=F), brow(k), ALU.add))

            def gin(r, cur):
                dve.wait_ge(s_aggn, r + 1)
                if r == 0:
                    dve.wait_ge(s_x, 48)
                chain(v.tensor_scalar(t2[:, :, :], cur[:, :, :], eps[:, r:r + 1], None, ALU.mult))
                v.tensor_tensor(t1[:, :, :], t2[:, :, :], agg_n[:, :, :], ALU.add).then_inc(s_in, 1)
                linear(2 * r)
                v.tensor_scalar(t1[:, :, :], t1[:, :, :], 0.0, None, ALU.max).then_inc(s_in, 1)
                linear(2 * r + 1)

            def layer_norm(o, i, k):
                chain(v.tensor_reduce(st1[:, :], flat(i), AX.X, ALU.add))
                chain(v.tensor_scalar(st1[:, :], st1[:, :], 1.0 / F, None, ALU.mult))
                chain(v.tensor_tensor(flat(i), flat(i), row(st1), ALU.subtract))
                chain(v.tensor_tensor(flat(t2), flat(i), flat(i), ALU.mult))
                chain(v.tensor_reduce(st1[:, :], flat(t2), AX.X, ALU.add))
                v.tensor_scalar(st1[:, :], st1[:, :], 1.0 / F, EPS, ALU.mult, ALU.add).then_inc(s_var, 1)
                dve.wait_ge(s_sqrt, k)
                chain(v.reciprocal(st2[:, :], st2[:, :]))
                return v.tensor_tensor(flat(o), flat(i), row(st2), ALU.mult)

            even = sorted_flag(dve)
            with dve.If(even > 0):
                window_chunk(0, 0)
                with dve.Fori(1, WCHUNKS - 1, 2) as n:
                    window_chunk(n, 1)
                    window_chunk(n + 1, 0)
                dense(0)
            with dve.Else():
                edges(0, 1)
                chain_in(v.tensor_copy(agg_n[:, :, :], PS[2][:, :].rearrange("p (b c) -> p b c", b=B)))
            gin(0, xn)
            v.tensor_scalar(hn[:, :, :], t1[:, :, :], 0.0, None, ALU.max).then_inc(s_h1, 1)
            dve.wait_ge(s_h1, 1)
            with dve.If(even > 0):
                dense(1)
            with dve.Else():
                edges(1, 1)
                chain_in(v.tensor_copy(agg_n[:, :, :], PS[2][:, :].rearrange("p (b c) -> p b c", b=B)))
            gin(1, hn)
            chain(v.tensor_reduce(st1[:, :], flat(t1), AX.X, ALU.max))
            v.tensor_tensor(flat(t1), flat(t1), row(st1), ALU.subtract).then_inc(s_sm, 1)
            dve.wait_ge(s_exp, 1)
            v.tensor_reduce(st1[:, :], flat(t2), AX.X, ALU.add).then_inc(s_sum, 1)
            dve.wait_ge(s_ln, 1)
            chain(v.tensor_tensor(flat(t1), flat(t1), row(st2), ALU.subtract))
            chain(v.tensor_tensor(t1[:, :, :], t1[:, :, :], xn[:, :, :], ALU.add))
            dve.wait_ge(s_tab, 16)
            chain(layer_norm(x2n, t1, 1))
            x3 = flat(x2n)
            chain(v.tensor_copy(xs[:, :, 0, :], x3))
            chain(v.tensor_tensor(flat(t1), x3, xs[:, :, 0, :], ALU.subtract))
            chain(v.tensor_copy(xs[:, :, 3, :], flat(t1)))
            for s, o in ((0, 1), (0, 2), (3, 4)):
                v.tensor_copy(xs[:, :, o, :], xs[:, :, s, :])
            v.tensor_tensor(xs[:, :, 5, :], flat(t1), xs[:, :, 3, :], ALU.subtract).then_inc(s_xs, 1)
            for g in range(B * L // 4):
                dve.wait_ge(s_xT, g + 1)
                v.tensor_copy(xsT[:, 4 * g:4 * g + 4, :],
                              PS[g % 2][:, :].bitcast(BF16)[0:KS, 0:4 * P].rearrange("k (c p) -> k c p", c=4)
                              ).then_inc(s_xTc, 1)
            for c in range(B * L):
                m = ROWS_P[c // L]
                dve.wait_ge(s_y, c + 1)
                if c >= 3:
                    dve.wait_ge(s_y_out[c % 3], 16 * (c // 3))
                s = 2 + 3 * (c % 2)
                if c % 2:
                    v.tensor_copy(y_sb[0:m, c % 3, YBANK:2 * YBANK], PS[s + 1][0:m, 0:YBANK])
                v.tensor_copy(y_sb[0:m, c % 3, 2 * YBANK:], PS[s + 2][0:m, 0:YBANK]).then_inc(s_yv, 1)
            dve.wait_ge(s_lT, 1)
            v.tensor_copy(logit[:, 0:512], PS[0][:, :]).then_inc(s_logit, 1)
            v.tensor_copy(logit[:, 512:], PS[1][:, 0:EDGE_COLS - 512]).then_inc(s_logit, 1)
            chain(v.tensor_tensor(flat(t2), x3, u_rows[:, 1:2, :].broadcast_to([P, B * L, F]), ALU.mult))
            chain(v.tensor_reduce(st2[:, :], flat(t2), AX.X, ALU.add))
            for k in range(3):
                dve.wait_ge(s_y_out[k], 16 * len(range(k, B * L, 3)))
            edges(2, 2)
            ps3 = lambda k: PS[k][:, :].rearrange("p (c f) -> p c f", f=F)
            chain(v.tensor_tensor(flat(t1), ps3(3), row(st2), ALU.mult))
            chain(v.tensor_tensor(flat(t1), flat(t1), ps3(2), ALU.add))
            chain(v.tensor_tensor(t1[:, :, :], t1[:, :, :], x2n[:, :, :], ALU.add))
            layer_norm(t1, t1, 2).then_inc(s_res, 1)

        @block.tensor
        def _(pe):
            mm, tr = nc.tensor.matmul, nc.tensor.transpose
            pe.wait_ge(s_prep, 1)
            mm(PS[2][:, 0:F], wa_rep[:, 0, :], ws_sb[:, :], start=True, stop=True)
            mm(PS[2][:, F:2 * F], wa_rep[:, 1, :], ws_sb[:, :], start=True, stop=True)
            mm(PS[2][0:KS, 64:65], ws_rep[:, :, :].rearrange("o s i -> o (s i)"), wa_sb[:, 0:1],
               start=True, stop=True)
            tr(PS[3][0:BASES, 0:RELS], comp_sb, ident[0:RELS, 0:RELS]).then_inc(s_u, 1)
            for g, (k, at, width) in enumerate(EDGE_T):
                if g >= 2:
                    pe.wait_ge(s_tc, g - 1)
                for q in range(width // P):
                    last = tr(PS[g % 2][:, q * P:(q + 1) * P], raw[:, k, at + q * P:at + (q + 1) * P], ident[:, :])
                last.then_inc(s_tr, 1)
            pe.wait_ge(s_uc, 3)
            mm(PS[3][0:RELS, 128:128 + F * F], compT, v_sb.rearrange("b i o -> b (i o)"),
               start=True, stop=True).then_inc(s_t, 1)
            pe.wait_ge(s_dt, 1)
            for k, (at, n) in enumerate(((0, 512), (512, TILES - 512))):
                mm(PS[4 + k][:, 0:n], check[:, 0, :], dst_t[:, at:at + n], start=True, stop=True)
                mm(PS[6 + k][:, 0:n], check[:, 1, :], dst_t[:, at:at + n], start=True, stop=False)
                last = mm(PS[6 + k][:, 0:n], check[:, 2, :], dst_t[:, at + 1:at + 1 + n], start=False, stop=True)
            last.then_inc(s_first, 1)
            pe.wait_ge(s_dmin, 1)
            tr(PS[2][0:1, 128:256], tmp2[:, 2:3], ident[:, :]).then_inc(s_dminT, 1)

            def window_chunk(n, k):
                pe.wait_ge(s_prev, n + 1)
                for j in range(CW):
                    s, used = j % SLOTS_W, freed(n, j)
                    pe.wait_ge(s_oh, n * CW + j + 1)
                    if used is not None:
                        pe.wait_ge(s_cop, used + 1)
                    has_prev = not isinstance(n, int) or n * CW + j >= 1
                    o = PS[s][:, 0:W * NC]
                    for q in range(G):
                        last = mm(o, win_lo[:, s, q, :], win_key[:, s, q, :], start=(q == 0),
                                  stop=(q == G - 1 and not has_prev))
                    if has_prev:
                        b = (j - 1) % SLOTS_W if j else (CW - 1) % SLOTS_W
                        last = mm(PS[s][:, 0:NC], win_lo[:, b, G - 1, :], win_prev[:, k, j, 0:NC],
                                  start=False, stop=True)
                    last.then_inc(s_win, 1)

            def dense(r):
                pe.wait_ge(s_xp, 4 * r + 4)
                if r == 0:
                    pe.wait_ge(s_cop, WINDOWS)
                for q in range(NB):
                    n = min(512, NODES - q * 512)
                    for c in range(NC):
                        last = mm(PS[q][0:3 * F, 0:n], x_parts[:, c, :, :].rearrange("p s f -> p (s f)"),
                                  counts[:, c, q * 512:q * 512 + n], start=(c == 0), stop=(c == NC - 1))
                    last.then_inc(s_den, 1)
                pe.wait_ge(s_dca, (r + 1) * len(range(0, NB, 2)))
                pe.wait_ge(s_dcv, (r + 1) * len(range(1, NB, 2)))
                for b in range(B):
                    m = ROWS_P[b]
                    for l in range(L):
                        at = b * P * L + l
                        last = tr(PS[b][0:m, l * 3 * F:(l + 1) * 3 * F],
                                  sum_t[0:3 * F, at:at + (m - 1) * L + 1:L], ident[0:3 * F, 0:3 * F])
                last.then_inc(s_denT, 1)

            def edges(r, halves):
                for h in range(halves):
                    mm(PS[h][:, 0:HI], zeros[:, 0:P], zeros[:, 0:HI], start=True, stop=False)

                def chunk(n, k):
                    pe.wait_ge(s_ready[r], n + 1)
                    for j in range(CH):
                        for h in range(halves):
                            for q in range(3):
                                last = mm(PS[h][:, 0:HI], spread[:, k, j, 3 * h + q, :], oh_hi[:, k, j, 0:HI],
                                          start=False, stop=False)
                    last.then_inc(s_used[r], 1)

                with pe.Fori(0, CHUNKS, 2) as n:
                    chunk(n, 0)
                    chunk(n + 1, 1)
                for h in range(halves):
                    last = mm(PS[h][:, 0:HI], zeros[:, 0:P], zeros[:, 0:HI], start=False, stop=True)
                last.then_inc(s_agg[r], 1)
                pe.wait_ge(s_aggc[r], 1)
                for h in range(halves):
                    for b in range(B):
                        last = tr(PS[2 + h][:, b * P:(b + 1) * P], agg_sb[:, h, b * P:(b + 1) * P], ident[:, :])
                last.then_inc(s_aggT[r], 1)

            n_in = [0]

            def linear(k):
                n_in[0] += 1
                pe.wait_ge(s_in, n_in[0])
                for b in range(B):
                    last = tr(PS[4][:, b * P:(b + 1) * P], t1[:, b, :], ident[:, :])
                last.then_inc(s_inT, 1)
                pe.wait_ge(s_hT, n_in[0])
                for b in range(B):
                    last = mm(PS[3][:, b * P:(b + 1) * P], hT[:, b, :], kron[:, k, :], start=True, stop=True)
                last.then_inc(s_lin, 1)

            even = sorted_flag(pe)
            pe.wait_ge(s_zero, 1)
            with pe.If(even > 0):
                window_chunk(0, 0)
                with pe.Fori(1, WCHUNKS - 1, 2) as n:
                    window_chunk(n, 1)
                    window_chunk(n + 1, 0)
                dense(0)
            with pe.Else():
                edges(0, 1)
            pe.wait_ge(s_kron, 16 * 32)
            linear(0)
            linear(1)
            with pe.If(even > 0):
                dense(1)
            with pe.Else():
                edges(1, 1)
            linear(2)
            linear(3)
            pe.wait_ge(s_xs, 1)
            for g in range(B * L // 4):
                if g >= 2:
                    pe.wait_ge(s_xTc, g - 1)
                for q in range(4):
                    c = 4 * g + q
                    last = tr(PS[g % 2][:, :].bitcast(BF16)[0:KS, q * P:(q + 1) * P],
                              xs[:, c, :, :].rearrange("p s f -> p (s f)"), ident_bf[:, :])
                last.then_inc(s_xT, 1)
            pe.wait_ge(s_xTc, B * L // 4)
            pe.wait_ge(s_attr_used, ATTR_N)
            for b in range(EDGE_BLOCKS):
                last = tr(PS[b // 4][:, (b % 4) * P:(b % 4 + 1) * P], logit_raw[:, b * P:(b + 1) * P], ident[:, :])
            last.then_inc(s_lT, 1)
            for c in range(B * L):
                m = ROWS_P[c // L]
                if c >= 2:
                    pe.wait_ge(s_ya, c - 1)
                    pe.wait_ge(s_yv, c - 1)
                for q in range(3):
                    last = mm(PS[2 + 3 * (c % 2) + q][0:m, 0:YBANK], xsT[:, c, 0:m],
                              w_stack[:, q * YBANK:(q + 1) * YBANK], start=True, stop=True)
                last.then_inc(s_y, 1)
            pe.wait_ge(s_logit, 2)
            edges(2, 2)


EDGE_COLS = EDGE_BLOCKS * P
NO_KEY = 2000
ATTR_E = 16
ATTR_N = EDGE_COLS // ATTR_E
EDGE_T = [(k, at, min(512, EDGE_COLS - at)) for k in (2, 3, 0, 1) for at in range(0, EDGE_COLS, 512)]


def attr_rows(attr, sb, b, q):
    tiles = P if b < FULL_EB else LAST_T
    top = b * P * P
    yield (attr[top:top + tiles * P, :].rearrange("(t e) f -> t (e f)", e=P)[
        :, q * ATTR_E * F:(q + 1) * ATTR_E * F], sb[0:tiles, :])
    left = min(ATTR_E, LAST_E - q * ATTR_E)
    if b == FULL_EB and left > 0:
        at = top + tiles * P + q * ATTR_E
        yield attr[at:at + left, :].rearrange("(a e) f -> a (e f)", a=1), sb[tiles:tiles + 1, 0:left * F]


_INS = ['x', 'src', 'dst', 'edge_attr_16', 'edge_type_90', 'L0_gnn_eps1', 'L0_gnn_w1a', 'L0_gnn_b1a',
        'L0_gnn_w1b', 'L0_gnn_b1b', 'L0_gnn_eps2', 'L0_gnn_w2a', 'L0_gnn_b2a', 'L0_gnn_w2b',
        'L0_gnn_b2b', 'L1_gnn_Ws', 'L1_gnn_Wa', 'L1_gnn_weight', 'L1_gnn_w_comp']


def shape_constants():
    slots = np.zeros((KS, 3), np.float32)
    for s, part_of_w in enumerate((0, 1, 2, 0, 1, 0)):
        slots[s * F:(s + 1) * F, part_of_w] = 1
    check = np.zeros((P, 3, P), np.float32)
    check[0, 0, :] = 1
    check[np.arange(P), 1, np.arange(P)] = -1
    check[np.arange(1, P), 1, np.arange(P - 1)] = 1
    check[0, 2, P - 1] = 1
    return {
        "ident": np.eye(P, dtype=np.float32),
        "iota_hi": np.arange(HI).astype(np.float16),
        "lane_l": np.repeat(np.arange(L), F).astype(np.float16),
        "slots": slots,
        "check": check,
    }


def kernel(**inputs):
    import concourse.bacc as _bacc
    from concourse.bass_utils import run_bass_kernel_spmd as _run

    nc = _bacc.Bacc("TRN2", target_bir_lowering=False, num_devices=1)
    arrays, args = {}, []
    for name in _INS:
        a = np.ascontiguousarray(inputs[name])
        if a.ndim == 0 or name.startswith("L0_gnn_eps"):
            a = a.reshape(1)
        arrays[f"in_{name}"] = a
        args.append(nc.dram_tensor(f"in_{name}", a.shape, mybir.dt.from_np(a.dtype), kind="ExternalInput").ap())
    for name, a in shape_constants().items():
        arrays[f"const_{name}"] = a
        args.append(nc.dram_tensor(f"const_{name}", a.shape, mybir.dt.from_np(a.dtype), kind="ExternalInput").ap())
    args.append(nc.dram_tensor("out_0", (NODES, F), FP32, kind="ExternalOutput").ap())
    build_gnn(nc, *args)
    r = _run(nc, [arrays], core_ids=[0])
    return r.results[0]["out_0"]
```

```python
import numpy as np
import concourse.bass as bass
import concourse.mybir as mybir
from contextlib import ExitStack

FP32 = mybir.dt.float32
BF16 = mybir.dt.bfloat16
FP16 = mybir.dt.float16
I32 = mybir.dt.int32
ALU = mybir.AluOpType
ACT = mybir.ActivationFunctionType
AX = mybir.AxisListType

P = 128
NODES, F = 3125, 16
EDGES = 103125
RELS, BASES = 90, 30
L = 8
B = 4
NODES_PAD = B * P * L
HI = -(-NODES // L)
FULL = NODES // (P * L)
LAST_P = (NODES - FULL * P * L) // L
LAST_L = NODES - FULL * P * L - LAST_P * L
TILES = -(-EDGES // P)
EDGE_BLOCKS = -(-TILES // P)
FULL_EB = TILES // P
LAST_T = EDGES // P - FULL_EB * P
LAST_E = EDGES - (FULL_EB * P + LAST_T) * P
CH = 13
CHUNKS = TILES // CH
assert CHUNKS * CH == TILES and CHUNKS % 2 == 0
PAD_DST = 8 * (HI + 100)
YW = F + 1
SLOTS = 6
KS = SLOTS * F
YCOLS = RELS * YW
YBANK = YCOLS // 3
EPS = 1e-5
NC = -(-NODES // P)
G = 2
W = 12
WINDOWS = TILES // G
CW = 13
WCHUNKS = WINDOWS // CW
assert WCHUNKS * CW * G == TILES and WCHUNKS % 2 == 1
SLOTS_W = 7
LO_GROUPS = ((0, 4), (4, 7), (7, 10), (10, 13))
LO_T = G * max(b - a for a, b in LO_GROUPS)
assert LO_GROUPS[-1][1] == CW
QW = 6
PAIRS = 3
assert QW % PAIRS == 0
FX = F + 1
QT, DT = QW * G, (CW - QW) * G
KC = 4
HC = -(-NC // KC)
DSTS = NODES + W - 1
NB = -(-NODES // 512)
ROWS_P = [P] * FULL + [LAST_P + (LAST_L > 0)]


def node_rows(dram, sb):
    top = FULL * P * L
    mid = top + LAST_P * L
    yield dram[0:top, :].rearrange("(b p l) f -> p b (l f)", p=P, l=L), sb[:, 0:FULL, :]
    yield dram[top:mid, :].rearrange("(p l) f -> p (l f)", l=L), sb[0:LAST_P, FULL, :]
    yield (dram[mid:NODES, :].rearrange("(a l) f -> a (l f)", a=1),
           sb[LAST_P:LAST_P + 1, FULL, 0:LAST_L * F])


def edge_rows(dram, sb, w):
    top = FULL_EB * P * P
    mid = top + LAST_T * P
    yield dram[0:top, :].rearrange("(b t e) w -> t b (e w)", t=P, e=P), sb[:, 0:FULL_EB, :]
    yield dram[top:mid, :].rearrange("(t e) w -> t (e w)", e=P), sb[0:LAST_T, FULL_EB, :]
    yield (dram[mid:EDGES, :].rearrange("(a e) w -> a (e w)", a=1),
           sb[LAST_T:LAST_T + 1, FULL_EB, 0:LAST_E * w])


def build_gnn(nc, x, src, dst, attr, etype, eps1, w1a, b1a, w1b, b1b, eps2, w2a, b2a, w2b, b2b,
              ws, wa, weight, w_comp, ident_c, iota_hi_c, lane_l_c, slot_c, check_c, lane_c, out):
    h_tab = nc.dram_tensor("h_tab", [NODES_PAD, F], FP32, kind="Internal").ap()
    wp_tab = nc.dram_tensor("wp_tab", [3 * F * RELS, F], BF16, kind="Internal").ap()
    y_tab = nc.dram_tensor("y_tab", [sum(ROWS_P) * L * RELS, YW], FP32, kind="Internal").ap()

    x2_tab = nc.dram_tensor("x2_tab", [NODES_PAD, F], FP32, kind="Internal").ap()
    rem_tab = nc.dram_tensor("rem_tab", [EDGE_COLS * P], FP16, kind="Internal").ap()
    type_tab = nc.dram_tensor("type_tab", [EDGE_COLS * P], FP16, kind="Internal").ap()

    ctx = ExitStack()
    with ctx:
        def sb(name, shape, dt=FP32):
            return ctx.enter_context(nc.sbuf_tensor(name, shape, dt))

        def sem(name):
            return ctx.enter_context(nc.semaphore(name))

        arena = sb("arena", [P, NC * DSTS], BF16)
        counts = arena[:, :].rearrange("p (c d) -> p c d", c=NC)
        cursor = [0]

        def carve(shape, dt=FP32):
            two = 2 if dt in (FP32, I32) else 1
            n = int(np.prod(shape[1:])) * two
            at = cursor[0]
            cursor[0] += -(-n // 16) * 16
            assert cursor[0] <= NC * DSTS, cursor[0]
            a = arena[0:shape[0], at:at + n]
            return a if dt == BF16 else a.bitcast(dt)

        ident = sb("ident", [P, P])
        ident_bf = sb("ident_bf", [P, P], BF16)
        iota_hi = sb("iota_hi", [P, HI], FP16)
        iota_l = sb("iota_l", [P, L * F], FP16)
        slot_mask = sb("slot_mask", [KS, 3])
        kron = sb("kron", [P, 4, P])
        bias = sb("bias", [P, 4, F])
        eps = sb("eps", [P, 2])
        ws_sb = sb("ws_sb", [F, F])
        ws_rep = sb("ws_rep", [F, SLOTS, F])
        wa_sb = sb("wa_sb", [F, 3])
        wa_rep = sb("wa_rep", [F, 3, P])
        u_rows = sb("u_rows", [P, 3, F])
        u_src = sb("u_src", [KS, 1])
        u_part = sb("u_part", [KS, 4], BF16)
        w_stack = sb("w_stack", [KS, YCOLS], BF16)
        lane = sb("lane", [P, KC + L + 2])
        row_idx = sb("row_idx", [P, EDGE_COLS], I32)
        logit_raw = sb("logit_raw", [P, EDGE_COLS])
        attr_ring = sb("attr_ring", [P, 2, ATTR_E * F])
        key = sb("key", [P, TILES], FP16)
        low_prev = sb("low_prev", [P, WCHUNKS, CW * G + CW], FP16)
        local = sb("local", [P, TILES], FP16)
        group = sb("group", [P, WCHUNKS, QT], FP16)
        first = sb("first", [1, WCHUNKS, 16], I32)
        low_st = sb("low_st", [P, 2, CW * G + CW], FP16)
        key_st = sb("key_st", [P, 2, CW * G])
        prev_st = low_st[:, :, CW * G:]
        n_lo, n_key, n_prev = CW * G * P, SLOTS_W * G * W * NC, 2 * CW * NC
        window = sb("window", [P, n_lo + n_key + n_prev], BF16)
        win_lo = [window[:, a * G * P:b * G * P].rearrange("p (k t) -> p k t", k=P) for a, b in LO_GROUPS]
        win_key = window[:, n_lo:n_lo + n_key].rearrange("p (s g k) -> p s g k", s=SLOTS_W, g=G)
        win_prev = window[:, n_lo + n_key:].rearrange("p (k c w) -> p k c w", k=2, w=CW)
        flag_f = sb("flag_f", [1, 8])
        flag_i = sb("flag_i", [1, 1], I32)
        sum_t = window[:, :].bitcast(FP32)
        x_parts = sb("x_parts", [P, NC, 3, F], BF16)
        iota_w = x_parts[:, :, :, :].rearrange("p c s f -> p (c s f)").bitcast(FP16)[:, 0:NC * CW].rearrange(
            "p (c w) -> p c w", c=NC)
        idx_st = sb("idx_st", [P, 2, CH], I32)
        meta_st = sb("meta_st", [P, 2, 3, CH])
        xn = sb("xn", [P, B, L * F])
        hn = sb("hn", [P, B, L * F])
        x2n = hn
        t1 = sb("t1", [P, B, L * F])
        t2 = sb("t2", [P, B, L * F])
        agg_n = t1
        x_c = [t[:, :, :].rearrange("p b n -> p (b n)")[:, 0:NC * F].rearrange("p (c f) -> p c f", c=NC)
               for t in (hn, t2)]
        iota_t = t2[:, :, :].rearrange("p b n -> p (b n)").bitcast(FP16)[:, 0:P * LO_T].rearrange(
            "p (k t) -> p k t", k=P)
        hT = t2
        st1 = sb("st1", [P, B * L])
        st2 = sb("st2", [P, B * L])

        src_idx = carve([P, EDGE_COLS], I32)
        dst_hl = carve([P, 2 * EDGE_COLS], FP16).rearrange("p (k n) -> p k n", k=2)
        zeros = carve([P, HI + 1], BF16)
        base = cursor[0]
        ints = carve([P, 5 * EDGE_COLS], I32).rearrange("p (k b e) -> p k b e", k=5, e=P)
        src_i, dst_i, type_i, hi_i, lo_i = (ints[:, k] for k in range(5))
        raw = carve([P, 4 * EDGE_COLS]).rearrange("p (k n) -> p k n", k=4)
        SRC, ROW, DHI, DLO = range(4)
        dst_t = carve([P, EDGE_COLS])
        firsts = carve([P, TILES])
        src_digits = carve([P, 3 * TILES], I32).rearrange("p (k t) -> p k t", k=3)
        src_hi = carve([P, TILES])
        key_prev = carve([P, WINDOWS])
        digits = carve([P, 2 * EDGE_COLS], FP16).rearrange("p (k n) -> p k n", k=2)
        tmp = carve([P, TILES])
        tmp2 = carve([P, TILES])
        check = carve([P, 6 * P], FP16).rearrange("p (h k m) -> p h k m", h=2, k=3)
        w_lin = carve([F, 4 * F]).rearrange("i (k o) -> i k o", k=4)
        sel = carve([F, P]).rearrange("i (l f) -> i l f", l=L)
        comp_sb = carve([RELS, BASES])
        compT = carve([BASES, RELS])
        v_sb = carve([BASES, F * F]).rearrange("b (i o) -> b i o", i=F)
        t_rest = carve([RELS, F * F])
        t_parts = carve([RELS, 3 * F * F], BF16).rearrange("r (s m) -> r s m", s=3)
        cursor[0] = base
        logit = carve([P, EDGE_COLS])
        xs = carve([P, B * L * KS], BF16).rearrange("p (c s f) -> p c s f", c=B * L, s=SLOTS)
        xsT = carve([KS, B * L * P], BF16).rearrange("p (c n) -> p c n", c=B * L)
        at_y = cursor[0]
        y_sb = carve([P, 3 * YCOLS]).rearrange("p (k w) -> p k w", k=3)
        past_y = cursor[0]
        cursor[0] = at_y
        rows = carve([P, 2 * CH * YW]).rearrange("p (k c w) -> p k c w", k=2, c=CH)
        msg = carve([P, CH * 2 * F]).rearrange("p (c f) -> p c f", c=CH)
        rest = carve([P, CH * 2 * F]).rearrange("p (c f) -> p c f", c=CH)
        part = [carve([P, CH * 2 * F], BF16).rearrange("p (c f) -> p c f", c=CH) for _ in range(3)]
        scale = carve([P, CH])
        oh_hi = carve([P, 2 * CH * (HI + 1)], BF16).rearrange("p (k c h) -> p k c h", k=2, c=CH)
        oh_l = carve([P, CH * P], BF16).rearrange("p (c m) -> p c m", c=CH)
        agg_sb = carve([P, 2 * B * P]).rearrange("p (h n) -> p h n", h=2)
        spread = carve([P, 2 * CH * 6 * P], BF16).rearrange("p (k c q m) -> p k c q m", k=2, c=CH, q=6)
        cursor[0] = at_y
        sums = carve([2 * F, DSTS])
        loc_oh = carve([P, 2 * CW * G * W]).rearrange("p (k t w) -> p k t w", k=2, t=CW * G)
        pick = carve([P, 2 * QT * HC]).rearrange("p (k t h) -> p k t h", k=2, t=QT)
        assert cursor[0] <= past_y
        cursor[0] = past_y
        w_parts = carve([RELS, 3 * F * F], BF16).rearrange("r (s m) -> r s m", s=3)
        x2_parts = carve([P, HC * KC * 3 * FX], BF16).rearrange("p (h k s f) -> p h k s f", h=HC, k=KC, s=3)
        x2_c = carve([P, NC * FX]).rearrange("p (c f) -> p c f", c=NC)
        x2_rest = carve([P, NC * FX]).rearrange("p (c f) -> p c f", c=NC)
        spread_dig = carve([P, 2 * 2 * QT * P], FP16).rearrange("p (k d e) -> p k d e", k=2, d=2)
        src_oh = carve([P, 2 * KC * QT * P], BF16).rearrange("p (k c e) -> p k c e", k=2, c=KC)
        type_oh = carve([P, 2 * QT * P], BF16).rearrange("p (k e) -> p k e", k=2)
        distance = carve([P, QT * P], BF16)
        MW = 2 * F + 1
        mess = carve([P, 2 * CW * G * MW]).rearrange("p (k t w) -> p k t w", k=2, t=CW * G)
        picked = carve([P, 2 * G * HC * FX]).rearrange("p (k t h f) -> p k t h f", k=2, t=G, h=HC)
        prod = carve([P, 4 * G * F * F]).rearrange("p (t i o) -> p t i o", t=4 * G, i=F)
        x_src = carve([P, QT * FX]).rearrange("p (t f) -> p t f", t=QT)
        mscale = carve([P, CW * G])
        di_st = carve([P, 2 * DT], I32).rearrange("p (k t) -> p k t", k=2)
        lo_st = carve([P, 2 * CW * G]).rearrange("p (k t) -> p k t", k=2)
        lg_st = carve([P, 2 * CW * G]).rearrange("p (k t) -> p k t", k=2)
        gr_st = carve([P, 2 * QT]).rearrange("p (k t) -> p k t", k=2)

        PS = [ctx.enter_context(nc.psum_tensor(f"ps{k}", [P, 512], FP32)) for k in range(8)]

        s_const = sem("const_loaded")
        s_w = sem("weights_loaded")
        s_kron = sem("kron_loaded")
        s_x = sem("x_loaded")
        s_xc = sem("x_chunks_loaded")
        s_e = sem("edges_loaded")
        s_attr = [sem(f"attr_loaded{k}") for k in range(2)]
        s_attr_used = sem("attr_used")
        s_attr_sum = sem("attr_sum_step")
        s_pads = sem("pads_filled")
        s_dve = sem("dve_step")
        s_zero = sem("zeros_written")
        s_prep = sem("edges_split")
        s_rep = sem("small_operands_repeated")
        s_tr = sem("edges_transposed")
        s_tc = sem("edges_copied")
        s_u = sem("logit_vectors")
        s_uc = sem("logit_vectors_copied")
        s_t = sem("t_product")
        s_split_t = sem("t_split_step")
        s_t_out = sem("t_parts_written")
        s_w_in = sem("w_rel_loaded")
        s_dt = sem("dst_joined")
        s_firstc = sem("firsts_copied")
        s_int = sem("source_digit")
        s_intc = sem("source_digit_copied")
        s_first = sem("firsts_and_diffs")
        s_dmin = sem("diff_min")
        s_dminT = sem("diff_min_transposed")
        s_flag = sem("flag_written")
        s_tab = sem("h_written")
        s_aggn = sem("agg_in_node_layout")
        s_in = sem("linear_input")
        s_inT = sem("linear_input_transposed")
        s_hT = sem("linear_input_copied")
        s_lin = sem("linear_product")
        s_h1 = sem("hidden_written")
        s_sm = sem("shifted_logits")
        s_exp = sem("exp_done")
        s_sum = sem("exp_sum")
        s_ln = sem("ln_done")
        s_var = sem("variance")
        s_sqrt = sem("sqrt_done")
        s_lT = sem("edge_logits_transposed")
        s_xs = sem("x2_parts")
        s_xT = sem("x2_parts_transposed")
        s_xTc = sem("x2_parts_copied")
        s_y = sem("y_product")
        s_ya = sem("y_copied_by_act")
        s_yv = sem("y_copied_by_dve")
        s_y_out = [sem(f"y_written{k}") for k in range(3)]
        s_logit = sem("edge_logits_copied")
        s_iota = sem("iotas_spread")
        s_vector = sem("source_vector_step")
        s_dig = sem("digits_split")
        s_dig_out = sem("digits_written")
        s_x2 = sem("x2_ready")
        s_x2_out = sem("x2_written")
        s_x2c = sem("x2_chunks_loaded")
        s_wr = sem("w_rel_rows_loaded")
        s_dist = sem("type_distance")
        s_type = sem("type_one_hot_ready")
        s_mask = sem("gathered_x_masked")
        s_parts = sem("gather_tables_ready")
        s_bc = [sem(f"digits_spread{k}") for k in range(2)]
        s_ohT = sem("source_one_hots_ready")
        s_st3 = sem("chunk_staged")
        s_di = sem("row_indices_staged")
        s_pick = sem("picks_ready")
        s_g = sem("window_gathered")
        s_gc = sem("window_picked")
        s_w3 = sem("window_step")
        s_sc = sem("message_scale")
        s_r3 = [sem(f"y_rows_landed{k}") for k in range(2)]
        s_msg = sem("messages_ready")
        s_scat = sem("chunk_summed")
        s_c3 = sem("sums_copied")
        s_sT = sem("sums_transposed")
        s_s12 = sem("sums_by_node")
        s_res = sem("result")
        s_out = sem("out_written")
        s_begun = sem("gathers_begun")
        R = range(3)
        s_idx = [sem(f"idx_staged{r}") for r in R]
        s_meta = [sem(f"meta_staged{r}") for r in R]
        s_rows = [[sem(f"rows_landed{r}_{k}") for k in range(2)] for r in R]
        s_split = [sem(f"split_step{r}") for r in R]
        s_ready = [sem(f"operands_ready{r}") for r in R]
        s_used = [sem(f"operands_used{r}") for r in R]
        s_agg = [sem(f"agg_done{r}") for r in R]
        s_aggc = [sem(f"agg_copied{r}") for r in R]
        s_aggT = [sem(f"agg_transposed{r}") for r in R]
        s_keys = sem("keys_staged")
        s_prev = sem("prev_keys_ready")
        s_oh = sem("window_operands_ready")
        s_win = sem("window_product")
        s_cop = sem("window_copied")
        s_xp = sem("x_parts_ready")
        s_den = sem("dense_product")
        s_dca = sem("dense_copied_by_act")
        s_dcv = sem("dense_copied_by_dve")
        s_denT = sem("dense_transposed")

        block = ctx.enter_context(nc.Block())

        def sorted_flag(eng):
            eng.wait_ge(s_flag, 1)
            return eng.value_load(flag_i[0:1, 0:1], min_val=0, max_val=1)

        def low(t):
            t %= CW * G
            i = next(i for i, (a, b) in enumerate(LO_GROUPS) if t < b * G)
            return win_lo[i][:, :, t - LO_GROUPS[i][0] * G]

        def freed(n, j):
            if j >= SLOTS_W:
                return n * CW + j - SLOTS_W
            if isinstance(n, int) and n == 0:
                return None
            return (n - 1) * CW + (j + SLOTS_W if j + SLOTS_W < CW else j)

        @block.sync
        def _(sp):
            sp.wait_ge(s_pads, 4)
            for a, t in ((src, src_i), (dst, dst_i), (etype, type_i)):
                for d, s in edge_rows(a.rearrange("(e w) -> e w", w=1), t, 1):
                    sp.dma_start(s, d).then_inc(s_e, 16)
            sp.dma_start(ident[:, :], ident_c).then_inc(s_const, 16)
            sp.dma_start(iota_hi[:, :], iota_hi_c.partition_broadcast(P)).then_inc(s_const, 16)
            sp.dma_start(iota_l[:, :], lane_l_c.partition_broadcast(P)).then_inc(s_const, 16)
            sp.dma_start(slot_mask[:, :], slot_c).then_inc(s_const, 16)
            sp.dma_start(check, check_c).then_inc(s_const, 16)
            sp.dma_start(lane[:, :], lane_c).then_inc(s_const, 16)
            for d, s in node_rows(x, xn):
                sp.dma_start(s, d).then_inc(s_x, 16)
            sp.wait_ge(s_pads, 5)
            top = (NC - 1) * P
            sp.dma_start(x_c[0][:, 0:NC - 1, :], x[0:top, :].rearrange("(c p) f -> p c f", p=P)).then_inc(s_xc, 16)
            sp.dma_start(x_c[0][0:NODES - top, NC - 1, :], x[top:NODES, :]).then_inc(s_xc, 16)
            sp.wait_ge(s_dig, 2)
            for k, t in enumerate((rem_tab, type_tab)):
                sp.dma_start(t.rearrange("(b t e) -> t b e", t=P, e=P),
                             digits[:, k, :].rearrange("p (b e) -> p b e", e=P)).then_inc(s_dig_out, 16)
            sp.wait_ge(s_split_t, 4)
            for q in range(3):
                sp.dma_start(wp_tab.rearrange("(s i r) o -> s r i o", s=3, r=RELS)[q],
                             t_parts[:, q, :].rearrange("r (i o) -> r i o", i=F)).then_inc(s_t_out, 16)
            sp.wait_ge(s_t_out, 16 * 3)
            for k, q in enumerate(W_PARTS):
                sp.dma_start(w_stack[k * F:(k + 1) * F, :].rearrange("i (r w) -> i r w", w=YW)[:, :, 0:F],
                             wp_tab.rearrange("(s r i) o -> s i r o", s=3, i=F)[q]).then_inc(s_w_in, 16)
            for n in range(ATTR_N):
                b, q = divmod(n, P // ATTR_E)
                if n >= 2:
                    sp.wait_ge(s_attr_used, n - 1)
                for d, s in attr_rows(attr, attr_ring[:, n % 2, :], b, q):
                    sp.dma_start(s, d).then_inc(s_attr[n % 2], 16)
            sp.wait_ge(s_dig_out, 32)
            sp.wait_ge(s_xc, 32)
            even = sorted_flag(sp)
            sp.wait_ge(s_h1, 1)
            sp.dma_start(h_tab.rearrange("(b p l) f -> p b (l f)", p=P, l=L), hn[:, :, :]).then_inc(s_tab, 16)
            with sp.If(even > 0):
                sp.wait_ge(s_tab, 16)
                sp.wait_ge(s_xp, 4)
                sp.dma_start(x_c[1], h_tab[0:NC * P, :].rearrange("(c p) f -> p c f", p=P)).then_inc(s_xc, 16)
            sp.end_ifs()
            sp.wait_ge(s_x2, 1)
            sp.dma_start(x2_tab.rearrange("(b p l) f -> p b (l f)", p=P, l=L), x2n[:, :, :]).then_inc(s_x2_out, 16)
            sp.wait_ge(s_x2_out, 16)
            sp.dma_start(x2_c[:, :, 0:F], x2_tab[0:NC * P, :].rearrange("(c p) f -> p c f", p=P)).then_inc(s_x2c, 16)
            sp.dma_start(w_parts, wp_tab.rearrange("(s r i) o -> r s (i o)", s=3, i=F)).then_inc(s_wr, 16)

            def spread_digits(n, k):
                if not isinstance(n, int) or n >= 2:
                    sp.wait_ge(s_ohT, n - 1)
                    sp.wait_ge(s_dist, n - 1)
                for d, t in enumerate((rem_tab, type_tab)):
                    sp.dma_start(spread_dig[:, k, d, :],
                                 t[bass.ds(n * (CW * G * P), QT * P)].partition_broadcast(P)).then_inc(s_bc[k], 16)

            with sp.If(even > 0):
                spread_digits(0, 0)
            sp.end_ifs()
            yv = y_tab.rearrange("(p l r) w -> l p (r w)", l=L, r=RELS)
            for c in range(B * L):
                n = ROWS_P[c // L]
                sp.wait_ge(s_ya, c + 1)
                sp.wait_ge(s_yv, c + 1)
                sp.dma_start(yv[c % L, (c // L) * P:(c // L) * P + n], y_sb[0:n, c % 3, :]).then_inc(s_y_out[c % 3], 16)

            with sp.If(even > 0):
                spread_digits(1, 1)
                with sp.Fori(2, WCHUNKS - 1, 2) as n:
                    spread_digits(n, 0)
                    spread_digits(n + 1, 1)
                spread_digits(WCHUNKS - 1, 0)
            sp.end_ifs()
            sp.wait_ge(s_res, 1)
            for d, s in node_rows(out, t1):
                sp.dma_start(d, s).then_inc(s_out, 16)
            sp.wait_ge(s_out, 48)

        @block.gpsimd
        def _(pool):
            pool.wait_ge(s_uc, 2)
            for n in range(ATTR_N):
                landed = sum(16 * len(list(attr_rows(attr, attr_ring[:, 0, :], *divmod(m, P // ATTR_E))))
                             for m in range(n % 2, n + 1, 2))
                pool.wait_ge(s_attr[n % 2], landed)
                a3 = attr_ring[:, n % 2, :].rearrange("p (e f) -> p e f", f=F)
                pool.tensor_tensor(a3, a3, u_rows[:, 1:2, :].broadcast_to([P, ATTR_E, F]),
                                   ALU.mult).then_inc(s_attr_sum, 1)
                at, w = 4 * n + 1, F // 2
                while w > 1:
                    pool.wait_ge(s_attr_sum, at)
                    pool.tensor_tensor(a3[:, :, 0:w], a3[:, :, 0:w], a3[:, :, w:2 * w], ALU.add).then_inc(s_attr_sum, 1)
                    at, w = at + 1, w // 2
                pool.wait_ge(s_attr_sum, at)
                pool.tensor_tensor(logit_raw[:, n * ATTR_E:(n + 1) * ATTR_E], a3[:, :, 0], a3[:, :, 1],
                                   ALU.add).then_inc(s_attr_used, 1)

            def gather(r, n, k, table, width):
                pool.wait_ge(s_idx[r], n + 1)
                if not isinstance(n, int) or n >= 2:
                    pool.wait_ge(s_ready[r], n - 1)
                pool.sem_inc(s_begun, 1)
                for j in range(CH):
                    pool.indirect_dma_start(
                        rows[:, k, j, 0:width], None, table,
                        bass.IndirectOffsetOnAxis(ap=idx_st[:, k, j:j + 1], axis=0),
                    ).then_inc(s_rows[r][k], 16)

            def gathers(r, table, width):
                gather(r, 0, 0, table, width)
                gather(r, 1, 1, table, width)
                with pool.Fori(2, CHUNKS, 2) as n:
                    gather(r, n, 0, table, width)
                    gather(r, n + 1, 1, table, width)

            even = sorted_flag(pool)
            with pool.If(even < 1):
                gathers(0, x, F)
                pool.wait_ge(s_tab, 16)
                gathers(1, h_tab, F)
            pool.end_ifs()
            for k in range(3):
                pool.wait_ge(s_y_out[k], 16 * len(range(k, B * L, 3)))

            def gather_window_rows(n, k):
                pool.wait_ge(s_di, n + 1)
                if not isinstance(n, int) or n >= 2:
                    pool.wait_ge(s_scat, n - 1)
                pool.sem_inc(s_begun, 1)
                for j in range(DT):
                    pool.indirect_dma_start(
                        mess[:, k, QT + j, F:MW], None, y_tab,
                        bass.IndirectOffsetOnAxis(ap=di_st[:, k, j:j + 1], axis=0),
                    ).then_inc(s_r3[k], 16)

            with pool.If(even > 0):
                gather_window_rows(0, 0)
                gather_window_rows(1, 1)
                with pool.Fori(2, WCHUNKS - 1, 2) as n:
                    gather_window_rows(n, 0)
                    gather_window_rows(n + 1, 1)
                gather_window_rows(WCHUNKS - 1, 0)
            with pool.Else():
                gathers(2, y_tab, YW)

        @block.scalar
        def _(act):
            act.dma_start(ws_sb[:, :], ws).then_inc(s_w, 16)
            act.dma_start(wa_sb[:, :], wa.rearrange("a (k o) -> (a o) k", k=3),
                          allow_slow_non_contiguous=True).then_inc(s_w, 16)
            act.dma_start(comp_sb, w_comp).then_inc(s_w, 16)
            act.dma_start(v_sb, weight.rearrange("b i o -> (b i o)").rearrange(
                "(i b o) -> b i o", i=F, b=BASES)).then_inc(s_w, 16)
            for k, a in enumerate((eps1, eps2)):
                act.dma_start(eps[:, k:k + 1], a.partition_broadcast(P)).then_inc(s_w, 16)
            for k, a in enumerate((b1a, b1b, b2a, b2b)):
                act.dma_start(bias[:, k, :], a.partition_broadcast(P)).then_inc(s_w, 16)
            for k, a in enumerate((w1a, w1b, w2a, w2b)):
                act.dma_start(w_lin[:, k, :], a).then_inc(s_w, 16)

            into = {SRC: src_idx, ROW: row_idx[:, :], DHI: dst_hl[:, 0, :], DLO: dst_hl[:, 1, :]}
            for g, (k, at, width) in enumerate(EDGE_T):
                act.wait_ge(s_tr, g + 1)
                nc.scalar.copy(into[k][:, at:at + width], PS[g % 2][:, 0:width]).then_inc(s_tc, 1)
                if g == FIRSTS_AFTER:
                    act.wait_ge(s_first, 1)
                    nc.scalar.copy(firsts[:, 0:512], PS[4][:, :]).then_inc(s_firstc, 1)
                    nc.scalar.copy(firsts[:, 512:TILES], PS[5][:, 0:TILES - 512]).then_inc(s_firstc, 1)
            for q, t in enumerate((src_hi, group[:, :, :], low_prev[:, :, 0:CW * G])):
                act.wait_ge(s_int, q + 1)
                d = src_digits[:, q, :] if q == 0 else src_digits[:, q, :].rearrange(
                    "p (n t) -> p n t", n=WCHUNKS)[:, :, 0:t.shape[2]]
                nc.scalar.copy(t, d).then_inc(s_intc, 1)
            act.wait_ge(s_prep, 2)
            for k, t in enumerate((hi_i, type_i)):
                nc.scalar.copy(digits[:, k, :].rearrange("p (b e) -> p b e", e=P), t).then_inc(s_dig, 1)
            nc.scalar.copy(iota_t[:, :, :], iota_hi[:, 0:P].rearrange("p (k a) -> p k a", a=1)
                           .broadcast_to([P, P, LO_T])).then_inc(s_iota, 1)
            nc.scalar.copy(iota_w, iota_hi[:, 0:NC].rearrange("p (c a) -> p c a", a=1)
                           .broadcast_to([P, NC, CW])).then_inc(s_iota, 1)

            def stage(r, n, k, which):
                if not isinstance(n, int) or n >= 2:
                    act.wait_ge(s_rows[r][k], 8 * CH * (n - k))
                act.copy(idx_st[:, k, :], which[:, bass.ds(n * CH, CH)]).then_inc(s_idx[r], 1)
                if not isinstance(n, int) or n >= 2:
                    act.wait_ge(s_ready[r], n - 1)
                act.copy(meta_st[:, k, 0:2, :], dst_hl[:, :, bass.ds(n * CH, CH)]).then_inc(s_meta[r], 1)
                if r == 2:
                    act.copy(meta_st[:, k, 2, :], logit[:, bass.ds(n * CH, CH)]).then_inc(s_meta[r], 1)

            def stages(r, which):
                stage(r, 0, 0, which)
                stage(r, 1, 1, which)
                with act.Fori(2, CHUNKS, 2) as n:
                    stage(r, n, 0, which)
                    stage(r, n + 1, 1, which)

            def stage_keys(n, k):
                if not isinstance(n, int) or n >= 2:
                    act.wait_ge(s_oh, (n - 1) * CW)
                act.copy(low_st[:, k, :], low_prev[:, bass.ds(n, 1), :].rearrange("p a t -> p (a t)")).then_inc(s_keys, 1)
                act.copy(key_st[:, k, :], key[:, bass.ds(n * CW * G, CW * G)]).then_inc(s_keys, 1)

            def windows(n, k):
                _, at = nc.values_load_multi_w_load_instructions(
                    first[0:1, bass.ds(n, 1), 0:CW].rearrange("a n w -> a (n w)"),
                    engines=(mybir.EngineType.Activation,), min_val=0, max_val=NODES - 1,
                    skip_runtime_bounds_check_because="the flag is up only for node numbers")
                for j in range(CW):
                    act.wait_ge(s_win, n * CW + j + 1)
                    if not isinstance(n, int) or n * CW + j >= 1:
                        act.wait_ge(s_cop, n * CW + j)
                    nc.scalar.copy(counts[:, :, bass.ds(at[j], W)],
                                   PS[j % SLOTS_W][:, 0:W * NC].rearrange("p (d c) -> p c d", c=NC)).then_inc(s_cop, 1)
                    if j == CW // 2:
                        if not isinstance(n, int) or n + 2 < WCHUNKS:
                            stage_keys(n + 2, k)

            def dense_copy(r):
                for q in range(0, NB, 2):
                    act.wait_ge(s_den, (r * NB) + q + 1)
                    n = min(512, NODES - q * 512)
                    nc.scalar.copy(sum_t[0:3 * F, q * 512:q * 512 + n], PS[q][0:3 * F, 0:n]).then_inc(s_dca, 1)

            even = sorted_flag(act)
            with act.If(even > 0):
                act.wait_ge(s_tc, len(EDGE_T))
                stage_keys(0, 0)
                stage_keys(1, 1)
                windows(0, 0)
                with act.Fori(1, WCHUNKS - 3, 2) as n:
                    windows(n, 1)
                    windows(n + 1, 0)
                windows(WCHUNKS - 2, 1)
                windows(WCHUNKS - 1, 0)
                dense_copy(0)
                dense_copy(1)
            with act.Else():
                stages(0, src_idx)
                act.wait_ge(s_ready[0], CHUNKS)
                stages(1, src_idx)
                act.wait_ge(s_ready[1], CHUNKS)
            act.wait_ge(s_sm, 1)
            nc.scalar.activation(t2[:, :, :], t1[:, :, :], ACT.Exp).then_inc(s_exp, 1)
            act.wait_ge(s_sum, 1)
            nc.scalar.activation(st2[:, :], st1[:, :], ACT.Ln).then_inc(s_ln, 1)
            act.wait_ge(s_var, 1)
            nc.scalar.activation(st2[:, :], st1[:, :], ACT.Sqrt).then_inc(s_sqrt, 1)
            for c in range(B * L):
                m = ROWS_P[c // L]
                act.wait_ge(s_y, c + 1)
                if c >= 3:
                    act.wait_ge(s_y_out[c % 3], 16 * (c // 3))
                s = 2 + 3 * (c % 2)
                if c % 2 == 0:
                    nc.scalar.copy(y_sb[0:m, c % 3, YBANK:2 * YBANK], PS[s + 1][0:m, 0:YBANK])
                nc.scalar.copy(y_sb[0:m, c % 3, 0:YBANK], PS[s][0:m, 0:YBANK]).then_inc(s_ya, 1)
            act.wait_ge(s_logit, 2)

            def stage_chunk(n, k):
                if not isinstance(n, int) or n >= 2:
                    act.wait_ge(s_r3[k], 8 * DT * (n - k))
                act.copy(di_st[:, k, :], row_idx[:, bass.ds(n * (CW * G) + QT, DT)]).then_inc(s_di, 1)
                if not isinstance(n, int) or n >= 2:
                    act.wait_ge(s_msg, n - 1)
                act.copy(lo_st[:, k, :], local[:, bass.ds(n * (CW * G), CW * G)]).then_inc(s_st3, 1)
                act.copy(lg_st[:, k, :], logit[:, bass.ds(n * (CW * G), CW * G)]).then_inc(s_st3, 1)
                act.copy(gr_st[:, k, :], group[:, bass.ds(n, 1), :].rearrange("p a t -> p (a t)")).then_inc(s_st3, 1)

            def type_one_hot(n, k):
                act.wait_ge(s_bc[k], 16 * (n - k + 2))
                if not isinstance(n, int) or n >= 1:
                    act.wait_ge(s_type, n)
                nc.scalar.activation(distance, spread_dig[:, k, 1, :], ACT.Abs, bias=lane[:, KC + L:KC + L + 1]
                                     ).then_inc(s_dist, 1)
                if not isinstance(n, int) or n >= 2:
                    act.wait_ge(s_g, (n - 1) * QW)
                act.wait_ge(s_dist, n + 1)
                nc.scalar.activation(type_oh[:, k, :], distance, ACT.Relu, scale=-1.0,
                                     bias=lane[:, KC + L + 1:]).then_inc(s_type, 1)

            def copy_sums(n, k):
                _, at = nc.values_load_multi_w_load_instructions(
                    first[0:1, bass.ds(n, 1), 0:CW].rearrange("a n w -> a (n w)"),
                    engines=(mybir.EngineType.Activation,), min_val=0, max_val=NODES - 1,
                    skip_runtime_bounds_check_because="the flag is up only for node numbers")
                act.wait_ge(s_scat, n + 1)
                for j in range(CW):
                    o = PS[2 * PAIRS][0:2 * F, j * W:(j + 1) * W]
                    act.wait_ge(s_c3, n * CW + j + 1)
                    nc.scalar.activation(sums[:, bass.ds(at[j], 1)], o[:, 0:1], ACT.Identity,
                                         bias=sums[:, bass.ds(at[j], 1)])
                    nc.scalar.copy(sums[:, bass.ds(at[j] + 1, W - 1)], o[:, 1:W]).then_inc(s_c3, 1)

            with act.If(even > 0):
                type_one_hot(0, 0)
                for k in range(3):
                    act.wait_ge(s_y_out[k], 16 * len(range(k, B * L, 3)))
                stage_chunk(0, 0)
                stage_chunk(1, 1)
                type_one_hot(1, 1)
                with act.Fori(2, WCHUNKS - 1, 2) as n:
                    stage_chunk(n, 0)
                    type_one_hot(n, 0)
                    copy_sums(n - 2, 0)
                    stage_chunk(n + 1, 1)
                    type_one_hot(n + 1, 1)
                    copy_sums(n - 1, 1)
                stage_chunk(WCHUNKS - 1, 0)
                type_one_hot(WCHUNKS - 1, 0)
                copy_sums(WCHUNKS - 3, 0)
                copy_sums(WCHUNKS - 2, 1)
                copy_sums(WCHUNKS - 1, 0)
            with act.Else():
                stages(2, row_idx)
            act.wait_ge(s_var, 2)
            nc.scalar.activation(st2[:, :], st1[:, :], ACT.Sqrt).then_inc(s_sqrt, 1)

        @block.vector
        def _(dve):
            count = [0]
            v = nc.vector

            def chain(ins):
                count[0] += 1
                ins.then_inc(s_dve, 1)
                dve.wait_ge(s_dve, count[0])

            v.memset(dst_i[:, FULL_EB, :], PAD_DST).then_inc(s_pads, 1)
            v.memset(src_i[:, FULL_EB, :], 0).then_inc(s_pads, 1)
            v.memset(type_i[:, FULL_EB, :], 0).then_inc(s_pads, 1)
            v.memset(xn[:, FULL:, :], 0.0).then_inc(s_pads, 1)
            v.memset(x_c[0][:, NC - 1, :], 0.0).then_inc(s_pads, 1)
            v.memset(agg_n[:, FULL, :], 0.0)
            v.memset(key_prev[:, 0:1], NO_KEY)
            v.memset(zeros, 0.0).then_inc(s_zero, 1)
            dve.wait_ge(s_e, 16 * 9)
            raw3 = [raw[:, k, :].rearrange("p (b e) -> p b e", b=EDGE_BLOCKS) for k in range(4)]
            v.tensor_scalar(hi_i, dst_i, 3, None, ALU.arith_shift_right)
            v.tensor_scalar(lo_i, dst_i, L - 1, None, ALU.bitwise_and)
            chain(v.tensor_copy(raw3[SRC], src_i))
            v.tensor_copy(raw3[DHI], hi_i)
            v.tensor_copy(raw3[DLO], lo_i).then_inc(s_prep, 1)
            dve.wait_ge(s_w, 16 * 14)
            v.tensor_copy(ws_rep[:, :, :], ws_sb[:, :].rearrange("o (a i) -> o a i", a=1)
                          .broadcast_to([F, SLOTS, F]))
            v.tensor_copy(wa_rep[:, :, :], wa_sb[:, :].rearrange("o (k a) -> o k a", a=1)
                          .broadcast_to([F, 3, P]))
            dve.wait_ge(s_const, 16 * 6)
            v.tensor_copy(sel, ident[0:F, 0:F].rearrange("i (a f) -> i a f", a=1)
                          .broadcast_to([F, L, F])).then_inc(s_rep, 1)
            v.tensor_scalar(eps[:, :], eps[:, :], 1.0, None, ALU.add)
            dve.wait_ge(s_prep, 1)
            v.tensor_scalar(raw3[ROW], raw3[SRC], float(RELS), None, ALU.mult)
            chain(v.tensor_scalar(hi_i, src_i, KC * P - 1, None, ALU.bitwise_and))
            v.tensor_tensor(raw3[ROW], raw3[ROW], type_i, ALU.add).then_inc(s_prep, 1)
            dve.wait_ge(s_u, 1)
            v.tensor_copy(compT, PS[3][0:BASES, 0:RELS]).then_inc(s_uc, 1)
            v.tensor_copy(u_rows[:, :, :], PS[2][:, 0:3 * F].rearrange("p (k f) -> p k f", k=3)).then_inc(s_uc, 1)
            v.tensor_copy(u_src[:, :], PS[2][0:KS, 64:65]).then_inc(s_uc, 1)
            dve.wait_ge(s_uc, 3)
            for k in range(4):
                last = v.tensor_tensor(kron[:, k, :].rearrange("p (l o) -> p l o", l=L),
                                       PS[2][:, 192 + k * F:192 + (k + 1) * F].rearrange(
                                           "p (a o) -> p a o", a=1).broadcast_to([P, L, F]),
                                       lane[:, KC:KC + L].rearrange("p (l a) -> p l a", a=1).broadcast_to([P, L, F]), ALU.mult)
            last.then_inc(s_kron, 1)
            dve.wait_ge(s_t, 1)
            t_sum = PS[3][0:RELS, 128:128 + F * F]
            v.tensor_copy(t_parts[:, 0, :], t_sum).then_inc(s_split_t, 1)
            dve.wait_ge(s_split_t, 1)
            v.tensor_tensor(t_rest, t_sum, t_parts[:, 0, :], ALU.subtract).then_inc(s_split_t, 1)
            dve.wait_ge(s_split_t, 2)
            v.tensor_copy(t_parts[:, 1, :], t_rest).then_inc(s_split_t, 1)
            dve.wait_ge(s_split_t, 3)
            v.tensor_tensor(t_parts[:, 2, :], t_rest, t_parts[:, 1, :], ALU.subtract).then_inc(s_split_t, 1)

            dve.wait_ge(s_tc, len(EDGE_T) // 2)
            v.scalar_tensor_tensor(out=dst_t, in0=dst_hl[:, 0, :], scalar=float(L), in1=dst_hl[:, 1, :],
                                   op0=ALU.mult, op1=ALU.add).then_inc(s_dt, 1)
            dve.wait_ge(s_tc, len(EDGE_T) * 3 // 4)
            for q, shift in enumerate((7, 9)):
                v.tensor_scalar(src_digits[:, q, :], src_idx[:, 0:TILES], shift, None,
                                ALU.arith_shift_right).then_inc(s_int, 1)
            v.tensor_scalar(src_digits[:, 2, :], src_idx[:, 0:TILES], P - 1, None, ALU.bitwise_and).then_inc(s_int, 1)
            dve.wait_ge(s_first, 1)
            v.tensor_reduce(tmp2[:, 0:1], PS[6][:, :], AX.X, ALU.min)
            chain(v.tensor_reduce(tmp2[:, 1:2], PS[7][:, 0:TILES - 512], AX.X, ALU.min))
            v.tensor_reduce(tmp2[:, 2:3], tmp2[:, 0:2], AX.X, ALU.min).then_inc(s_dmin, 1)
            dve.wait_ge(s_dt, 1)
            dve.wait_ge(s_firstc, 2)
            w1 = lambda t: t.rearrange("p (g q) -> p g q", q=G)
            chain(v.tensor_tensor(w1(tmp), w1(dst_t[:, 0:TILES]),
                                  w1(firsts)[:, :, 0:1].broadcast_to([P, WINDOWS, G]), ALU.subtract))
            chain(v.tensor_scalar(local[:, :], tmp, float(NO_KEY // NC), None, ALU.min))
            chain(v.tensor_scalar(tmp, tmp, float(NO_KEY // NC), float(NC), ALU.min, ALU.mult))
            dve.wait_ge(s_intc, 3)
            chain(v.tensor_tensor(key[:, :], tmp, src_hi, ALU.add))
            gp = WINDOWS - 1
            before = lambda t: w1(t)[:, 0:gp, G - 1]
            chain(v.tensor_tensor(tmp[:, 0:gp], before(dst_t[:, 0:TILES]), w1(firsts)[:, 1:, 0], ALU.is_equal))
            chain(v.tensor_scalar(tmp[:, 0:gp], tmp[:, 0:gp], -float(NO_KEY), float(NO_KEY), ALU.mult, ALU.add))
            chain(v.tensor_tensor(key_prev[:, 1:], tmp[:, 0:gp], before(src_hi), ALU.add))
            v.tensor_copy(low_prev[:, :, CW * G:], key_prev.rearrange("p (n w) -> p n w", n=WCHUNKS))
            chain(v.tensor_copy(first[0:1, :, 0:CW], firsts[0:1, 0:TILES].rearrange(
                "a (n w q) -> a n w q", w=CW, q=G)[:, :, :, 0]))
            f1 = firsts[0:1, :]
            chain(v.tensor_tensor(tmp[0:1, 0:TILES - 1], f1[:, 1:], f1[:, 0:TILES - 1], ALU.subtract))
            chain(v.tensor_reduce(flag_f[:, 0:1], tmp[0:1, 0:TILES - 1], AX.X, ALU.min))
            fw = w1(f1)[:, :, 0]
            chain(v.tensor_tensor(tmp[0:1, 0:gp], fw[:, 1:], fw[:, 0:gp], ALU.subtract))
            v.tensor_scalar(tmp[0:1, gp:gp + 1], fw[:, gp:gp + 1], -1.0, float(NODES), ALU.mult, ALU.add)
            chain(v.tensor_scalar(flag_f[:, 1:2], fw[:, 0:1], 0.0, None, ALU.is_equal))
            chain(v.tensor_reduce(flag_f[:, 2:3], tmp[0:1, 0:WINDOWS], AX.X, ALU.max))
            dve.wait_ge(s_dminT, 1)
            chain(v.tensor_reduce(flag_f[:, 3:4], PS[2][0:1, 128:256], AX.X, ALU.min))
            v.tensor_scalar(flag_f[:, 4:5], flag_f[:, 0:1], 1.0, None, ALU.is_ge)
            v.tensor_scalar(flag_f[:, 5:6], flag_f[:, 2:3], float(W - 1), None, ALU.is_le)
            chain(v.tensor_scalar(flag_f[:, 6:7], flag_f[:, 3:4], 0.0, None, ALU.is_ge))
            chain(v.tensor_tensor(flag_f[:, 4:5], flag_f[:, 4:5], flag_f[:, 5:6], ALU.mult))
            chain(v.tensor_tensor(flag_f[:, 6:7], flag_f[:, 6:7], flag_f[:, 1:2], ALU.mult))
            chain(v.tensor_tensor(flag_f[:, 4:5], flag_f[:, 4:5], flag_f[:, 6:7], ALU.mult))
            v.tensor_copy(ident_bf[:, :], ident[:, :])
            dve.wait_ge(s_iota, 2)
            dve.wait_ge(s_dig_out, 32)
            dve.wait_ge(s_t_out, 16 * 3)
            v.tensor_copy(flag_i[:, :], flag_f[:, 4:5]).then_inc(s_flag, 1)

            def source_vector():
                def then(ins, i):
                    ins.then_inc(s_vector, 1)
                    dve.wait_ge(s_vector, i)

                then(v.tensor_copy(u_part[:, 0:1], u_src[:, :]), 1)
                then(v.tensor_tensor(u_src[:, :], u_src[:, :], u_part[:, 0:1], ALU.subtract), 2)
                then(v.tensor_copy(u_part[:, 1:2], u_src[:, :]), 3)
                then(v.tensor_tensor(u_part[:, 2:3], u_src[:, :], u_part[:, 1:2], ALU.subtract), 4)
                then(v.tensor_scalar(u_part[:, 3:4], u_part[:, 0:1], slot_mask[:, 0:1], None, ALU.mult), 5)
                for q in (1, 2):
                    then(v.scalar_tensor_tensor(out=u_part[:, 3:4], in0=u_part[:, q:q + 1],
                                                scalar=slot_mask[:, q:q + 1], in1=u_part[:, 3:4],
                                                op0=ALU.mult, op1=ALU.add), 5 + q)

            def window_chunk(n, k):
                dve.wait_ge(s_keys, 2 * n + 2)
                if not isinstance(n, int) or n >= 2:
                    dve.wait_ge(s_win, (n - 1) * CW)
                v.tensor_tensor(win_prev[:, k], iota_w, prev_st[:, k, :].rearrange("p (a w) -> p a w", a=1)
                                .broadcast_to([P, NC, CW]), ALU.is_equal).then_inc(s_prev, 1)
                for j in range(CW):
                    s, used = j % SLOTS_W, freed(n, j)
                    for i, (a, b) in enumerate(LO_GROUPS):
                        if j == a:
                            if not isinstance(n, int) or n >= 1:
                                dve.wait_ge(s_win, (n - 1) * CW + b + 1)
                            t = (b - a) * G
                            v.tensor_tensor(win_lo[i], iota_t[:, :, 0:t], low_st[:, k, a * G:b * G].rearrange(
                                "p (a t) -> p a t", a=1).broadcast_to([P, P, t]), ALU.is_equal)
                    if used is not None:
                        dve.wait_ge(s_win, used + 1)
                    for q in range(G):
                        last = v.tensor_scalar(win_key[:, s, q, :], iota_hi[:, 0:W * NC],
                                               key_st[:, k, G * j + q:G * j + q + 1], None, ALU.is_equal)
                    last.then_inc(s_oh, 1)

            def dense(r):
                xp = [x_parts[:, :, q, :] for q in range(3)]
                if r == 0:
                    source_vector()
                dve.wait_ge(s_xc, 32 + 16 * r)
                v.tensor_copy(xp[0], x_c[r]).then_inc(s_xp, 1)
                dve.wait_ge(s_xp, 4 * r + 1)
                v.tensor_tensor(x_c[r], x_c[r], xp[0], ALU.subtract).then_inc(s_xp, 1)
                dve.wait_ge(s_xp, 4 * r + 2)
                v.tensor_copy(xp[1], x_c[r]).then_inc(s_xp, 1)
                dve.wait_ge(s_xp, 4 * r + 3)
                v.tensor_tensor(xp[2], x_c[r], xp[1], ALU.subtract).then_inc(s_xp, 1)
                if r == 0:
                    dve.wait_ge(s_win, WINDOWS)
                    v.memset(sum_t[0:3 * F, NODES:NODES + W], 0.0)
                for b in range(B):
                    q = 2 * b + 1
                    if q < NB:
                        dve.wait_ge(s_den, r * NB + q + 1)
                        n = min(512, NODES - q * 512)
                        v.tensor_copy(sum_t[0:3 * F, q * 512:q * 512 + n], PS[q][0:3 * F, 0:n]).then_inc(s_dcv, 1)
                    dve.wait_ge(s_denT, r * B + b + 1)
                    m = ROWS_P[b]
                    last = v.tensor_reduce(agg_n[0:m, b, :].rearrange("p (l f) -> p l f", f=F),
                                           PS[b][0:m, 0:L * 3 * F].rearrange("p (l s f) -> p l f s", s=3, f=F),
                                           AX.X, ALU.add)
                chain_in(last)

            def edge_chunk(r, n, k):
                w = F if r < 2 else 2 * F
                steps = 4 if r < 2 else 6
                got = rows[:, k, :, :]

                def split(ins, i):
                    ins.then_inc(s_split[r], 1)
                    return n * steps + i + 1

                dve.wait_ge(s_meta[r], (n + 1) * (2 if r == 2 else 1))
                if not isinstance(n, int) or n >= 2:
                    dve.wait_ge(s_used[r], n - 1)
                for j in range(CH):
                    v.tensor_scalar(oh_hi[:, k, j, 0:HI], iota_hi[:, :], meta_st[:, k, 0, j:j + 1],
                                    None, ALU.is_equal)
                if not isinstance(n, int) or n >= 1:
                    dve.wait_ge(s_ready[r], n)
                for j in range(CH):
                    v.tensor_scalar(oh_l[:, j, :], iota_l[:, :], meta_st[:, k, 1, j:j + 1],
                                    None, ALU.is_equal)
                dve.wait_ge(s_rows[r][k], 8 * CH * (n - k + 2))
                i = 0
                val = got[:, :, 0:F]
                if r == 2:
                    at = split(v.tensor_tensor(scale, got[:, :, F], meta_st[:, k, 2, :], ALU.add), 0)
                    dve.wait_ge(s_split[r], at)
                    v.tensor_tensor(msg[:, :, 0:F], val, scale.rearrange("p (c a) -> p c a", a=1)
                                    .broadcast_to([P, CH, F]), ALU.mult)
                    at = split(v.tensor_copy(msg[:, :, F:2 * F], val), 1)
                    dve.wait_ge(s_split[r], at)
                    val, i = msg, 2
                p0, p1, p2 = (q[:, :, 0:w] for q in part)
                rs = rest[:, :, 0:w]
                dve.wait_ge(s_split[r], split(v.tensor_copy(p0, val), i))
                dve.wait_ge(s_split[r], split(v.tensor_tensor(rs, val, p0, ALU.subtract), i + 1))
                dve.wait_ge(s_split[r], split(v.tensor_copy(p1, rs), i + 2))
                dve.wait_ge(s_split[r], split(v.tensor_tensor(p2, rs, p1, ALU.subtract), i + 3))
                oh4 = oh_l.rearrange("p c (l f) -> p c l f", f=F)
                for h in range(w // F):
                    for q in range(3):
                        o = spread[:, k, :, 3 * h + q, :].rearrange("p c (l f) -> p c l f", f=F)
                        s = part[q][:, :, h * F:(h + 1) * F].rearrange("p c (a f) -> p c a f", a=1)
                        last = v.tensor_tensor(o, oh4, s.broadcast_to([P, CH, L, F]), ALU.mult)
                last.then_inc(s_ready[r], 1)

            def edges(r, halves):
                v.memset(agg_sb[:, :, HI:], 0.0)
                edge_chunk(r, 0, 0)
                edge_chunk(r, 1, 1)
                with dve.Fori(2, CHUNKS, 2) as n:
                    edge_chunk(r, n, 0)
                    edge_chunk(r, n + 1, 1)
                dve.wait_ge(s_agg[r], 1)
                for h in range(halves):
                    last = v.tensor_copy(agg_sb[:, h, 0:HI], PS[h][:, 0:HI])
                last.then_inc(s_aggc[r], 1)
                dve.wait_ge(s_aggT[r], 1)

            flat = lambda t: t[:, :, :].rearrange("p b (l f) -> p (b l) f", f=F)
            row = lambda s: s[:, :].rearrange("p (c a) -> p c a", a=1).broadcast_to([P, B * L, F])
            brow = lambda k: bias[:, k:k + 1, :].broadcast_to([P, B * L, F])
            n_in = [0]

            def chain_in(ins):
                ins.then_inc(s_aggn, 1)

            def linear(k):
                n_in[0] += 1
                dve.wait_ge(s_inT, n_in[0])
                v.tensor_copy(hT[:, :, :], PS[4][:, :].rearrange("p (b n) -> p b n", b=B)).then_inc(s_hT, 1)
                dve.wait_ge(s_lin, n_in[0])
                chain(v.tensor_tensor(flat(t1), PS[3][:, :].rearrange("p (c f) -> p c f", f=F), brow(k), ALU.add))

            def gin(r, cur):
                dve.wait_ge(s_aggn, r + 1)
                if r == 0:
                    dve.wait_ge(s_x, 48)
                v.scalar_tensor_tensor(out=t1[:, :, :], in0=cur[:, :, :], scalar=eps[:, r:r + 1], in1=agg_n[:, :, :],
                                       op0=ALU.mult, op1=ALU.add).then_inc(s_in, 1)
                linear(2 * r)
                v.tensor_scalar(t1[:, :, :], t1[:, :, :], 0.0, None, ALU.max).then_inc(s_in, 1)
                linear(2 * r + 1)

            def layer_norm(o, i, k):
                chain(v.tensor_reduce(st1[:, :], flat(i), AX.X, ALU.add))
                chain(v.tensor_scalar(st1[:, :], st1[:, :], 1.0 / F, None, ALU.mult))
                chain(v.tensor_tensor(flat(i), flat(i), row(st1), ALU.subtract))
                chain(v.tensor_tensor(flat(t2), flat(i), flat(i), ALU.mult))
                chain(v.tensor_reduce(st1[:, :], flat(t2), AX.X, ALU.add))
                v.tensor_scalar(st1[:, :], st1[:, :], 1.0 / F, EPS, ALU.mult, ALU.add).then_inc(s_var, 1)
                dve.wait_ge(s_sqrt, k)
                chain(v.reciprocal(st2[:, :], st2[:, :]))
                return v.tensor_tensor(flat(o), flat(i), row(st2), ALU.mult)

            even = sorted_flag(dve)
            with dve.If(even > 0):
                window_chunk(0, 0)
                window_chunk(1, 1)
                with dve.Fori(2, WCHUNKS - 1, 2) as n:
                    window_chunk(n, 0)
                    window_chunk(n + 1, 1)
                window_chunk(WCHUNKS - 1, 0)
                dense(0)
            with dve.Else():
                source_vector()
                edges(0, 1)
                chain_in(v.tensor_copy(agg_n[:, :, :], PS[2][:, :].rearrange("p (b c) -> p b c", b=B)))
            gin(0, xn)
            v.tensor_scalar(hn[:, :, :], t1[:, :, :], 0.0, None, ALU.max).then_inc(s_h1, 1)
            dve.wait_ge(s_h1, 1)
            with dve.If(even > 0):
                dense(1)
            with dve.Else():
                edges(1, 1)
                chain_in(v.tensor_copy(agg_n[:, :, :], PS[2][:, :].rearrange("p (b c) -> p b c", b=B)))
            gin(1, hn)
            chain(v.tensor_reduce(st1[:, :], flat(t1), AX.X, ALU.max))
            v.tensor_tensor(flat(t1), flat(t1), row(st1), ALU.subtract).then_inc(s_sm, 1)
            dve.wait_ge(s_exp, 1)
            v.tensor_reduce(st1[:, :], flat(t2), AX.X, ALU.add).then_inc(s_sum, 1)
            dve.wait_ge(s_ln, 1)
            chain(v.tensor_tensor(flat(t1), flat(t1), row(st2), ALU.subtract))
            chain(v.tensor_tensor(t1[:, :, :], t1[:, :, :], xn[:, :, :], ALU.add))
            dve.wait_ge(s_tab, 16)
            layer_norm(x2n, t1, 1).then_inc(s_x2, 1)
            dve.wait_ge(s_x2, 1)
            dve.wait_ge(s_w_in, 16 * SLOTS)
            v.tensor_copy(w_stack[:, :].rearrange("k (r w) -> k r w", w=YW)[:, :, F:YW],
                          u_part[:, 3:4].rearrange("p (a b) -> p a b", a=1).broadcast_to([KS, RELS, 1]))
            x3 = flat(x2n)
            chain(v.tensor_copy(xs[:, :, 0, :], x3))
            chain(v.tensor_tensor(flat(t1), x3, xs[:, :, 0, :], ALU.subtract))
            chain(v.tensor_copy(xs[:, :, 3, :], flat(t1)))
            for s, o in ((0, 1), (0, 2), (3, 4)):
                v.tensor_copy(xs[:, :, o, :], xs[:, :, s, :])
            v.tensor_tensor(xs[:, :, 5, :], flat(t1), xs[:, :, 3, :], ALU.subtract).then_inc(s_xs, 1)
            for g in range(B * L // 4):
                dve.wait_ge(s_xT, g + 1)
                v.tensor_copy(xsT[:, 4 * g:4 * g + 4, :],
                              PS[g % 2][:, :].bitcast(BF16)[0:KS, 0:4 * P].rearrange("k (c p) -> k c p", c=4)
                              ).then_inc(s_xTc, 1)
            xg = [x2_parts.rearrange("p h k s f -> p (h k) s f")[:, 0:NC, q, :] for q in range(3)]

            def table_step(i):
                if i == 0:
                    ins = v.memset(x2_parts, 0.0)
                elif i == 1:
                    dve.wait_ge(s_x2c, 16)
                    ins = v.tensor_tensor(x2_rest[:, :, 0:F], x2_c[:, :, 0:F],
                                          u_rows[:, 0:1, :].broadcast_to([P, NC, F]), ALU.mult)
                elif i == 2:
                    ins = v.tensor_reduce(x2_c[:, :, F], x2_rest[:, :, 0:F], AX.X, ALU.add)
                elif i == 3:
                    ins = v.tensor_copy(xg[0], x2_c)
                elif i == 4:
                    ins = v.tensor_tensor(x2_rest, x2_c, xg[0], ALU.subtract)
                elif i == 5:
                    ins = v.tensor_copy(xg[1], x2_rest)
                else:
                    ins = v.tensor_tensor(xg[2], x2_rest, xg[1], ALU.subtract)
                ins.then_inc(s_parts, 1)

            for c in range(B * L):
                m = ROWS_P[c // L]
                dve.wait_ge(s_y, c + 1)
                if c >= 3:
                    dve.wait_ge(s_y_out[c % 3], 16 * (c // 3))
                s = 2 + 3 * (c % 2)
                if c % 2:
                    v.tensor_copy(y_sb[0:m, c % 3, YBANK:2 * YBANK], PS[s + 1][0:m, 0:YBANK])
                v.tensor_copy(y_sb[0:m, c % 3, 2 * YBANK:], PS[s + 2][0:m, 0:YBANK]).then_inc(s_yv, 1)
                if c == 1:
                    dve.wait_ge(s_lT, 1)
                    v.tensor_copy(logit[:, 0:512], PS[0][:, :]).then_inc(s_logit, 1)
                elif c == 2:
                    v.tensor_copy(logit[:, 512:], PS[1][:, 0:EDGE_COLS - 512]).then_inc(s_logit, 1)
                elif c == 3:
                    chain(v.tensor_tensor(flat(t2), x3, u_rows[:, 2:3, :].broadcast_to([P, B * L, F]), ALU.mult))
                elif c == 4:
                    chain(v.tensor_reduce(st2[:, :], flat(t2), AX.X, ALU.add))
                elif c - 5 in range(7):
                    if c > 5:
                        dve.wait_ge(s_parts, c - 5)
                    table_step(c - 5)

            def source_one_hots(n, k, i):
                if i == 0:
                    dve.wait_ge(s_bc[k], 16 * (n - k + 2))
                    if not isinstance(n, int) or n >= 2:
                        dve.wait_ge(s_g, (n - 1) * QW)
                for c in range(KC)[-(-KC * i // PAIRS):-(-KC * (i + 1) // PAIRS)]:
                    last = v.tensor_scalar(src_oh[:, k, c, :], spread_dig[:, k, 0, :], lane[:, c:c + 1],
                                           None, ALU.is_equal)
                if i == PAIRS - 1:
                    last.then_inc(s_ohT, 1)

            STEPS = QW + QW // 2

            def messages(n, k, ahead=True):
                dve.wait_ge(s_st3, 3 * n + 3)
                if not isinstance(n, int) or n >= 2:
                    dve.wait_ge(s_scat, n - 1)
                iota3 = lambda m, t: iota_hi[:, 0:m].rearrange("p (a w) -> p a w", a=1).broadcast_to([P, t, m])
                wide = lambda a, t, m: a.rearrange("p (t a) -> p t a", a=1).broadcast_to([P, t, m])
                v.tensor_tensor(pick[:, k, :, :], iota3(HC, QT), wide(gr_st[:, k, :], QT, HC), ALU.is_equal).then_inc(s_pick, 1)
                v.tensor_tensor(loc_oh[:, k, :, :], iota3(W, CW * G), wide(lo_st[:, k, :], CW * G, W), ALU.is_equal)
                dve.wait_ge(s_pick, n + 1)

                order = {}

                def step(name, w, ins):
                    order[name, w] = len(order) + 1
                    ins.then_inc(s_w3, 1)

                def after(name, w):
                    dve.wait_ge(s_w3, n * STEPS + order[name, w])

                tiles = lambda w: slice(G * w, G * (w + 1))

                def mask(w):
                    dve.wait_ge(s_g, n * QW + w + 1)
                    g4 = PS[w % PAIRS][:, 0:G * HC * FX].rearrange("p (t h f) -> p t h f", t=G, h=HC)
                    m4 = pick[:, k, tiles(w), :].rearrange("p t (h a) -> p t h a", a=1)
                    v.tensor_tensor(picked[:, w % 2], g4, m4.broadcast_to([P, G, HC, FX]), ALU.mult).then_inc(s_mask, 1)

                def pick_x(w):
                    dve.wait_ge(s_mask, n * QW + w + 1)
                    step("pick", w, v.tensor_reduce(x_src[:, tiles(w), :], picked[:, w % 2].rearrange(
                        "p t h f -> p t f h"), AX.X, ALU.add))

                def multiply(w):
                    after("pick", w)
                    x4 = x_src[:, tiles(w), 0:F].rearrange("p t (i a) -> p t i a", a=1)
                    v.tensor_tensor(prod[:, G * (w % 4):G * (w % 4 + 1)], PS[PAIRS + w % PAIRS][:, :].rearrange(
                        "p (t i o) -> p t i o", t=G, i=F), x4.broadcast_to([P, G, F, F]), ALU.mult).then_inc(s_gc, 1)

                def fold(w):
                    dve.wait_ge(s_gc, n * QW + w + 1)
                    at = G * ((w - 1) % 4)
                    step("fold", w, v.tensor_reduce(mess[:, k, G * (w - 1):G * (w + 1), F:2 * F], prod[:, at:at + 2 * G]
                                                    .rearrange("p t i o -> p t o i"), AX.X, ALU.add))

                mask(0)
                pick_x(0)
                for w in range(QW):
                    if w + 1 < QW:
                        mask(w + 1)
                    multiply(w)
                    if w + 1 < QW:
                        pick_x(w + 1)
                    if w >= 2 and w % 2 == 0:
                        fold(w - 1)
                    if ahead and w < PAIRS:
                        source_one_hots(n + 1, 1 - k, w)
                v.tensor_tensor(mscale[:, 0:QT], x_src[:, :, F], lg_st[:, k, 0:QT], ALU.add).then_inc(s_sc, 1)
                fold(QW - 1)
                dve.wait_ge(s_r3[k], 8 * DT * (n - k + 2))
                v.tensor_tensor(mscale[:, QT:], mess[:, k, QT:, 2 * F], lg_st[:, k, QT:], ALU.add).then_inc(s_sc, 1)
                for i, (t, width) in enumerate(((slice(0, QT), QT), (slice(QT, CW * G), DT))):
                    dve.wait_ge(s_sc, 2 * n + 1 + i)
                    if i == 0:
                        dve.wait_ge(s_w3, (n + 1) * STEPS)
                    last = v.tensor_tensor(mess[:, k, t, 0:F], mess[:, k, t, F:2 * F], wide(mscale[:, t], width, F), ALU.mult)
                last.then_inc(s_msg, 1)

            s12 = (t1, t2)
            with dve.If(even > 0):
                for i in range(PAIRS):
                    source_one_hots(0, 0, i)
                for k in range(3):
                    dve.wait_ge(s_y_out[k], 16 * len(range(k, B * L, 3)))
                v.memset(sums[:, 0:1], 0.0).then_inc(s_c3, 1)
                messages(0, 0)
                messages(1, 1)
                with dve.Fori(2, WCHUNKS - 1, 2) as n:
                    messages(n, 0)
                    messages(n + 1, 1)
                messages(WCHUNKS - 1, 0, ahead=False)
                v.memset(t1[:, FULL, :], 0.0)
                v.memset(t2[:, FULL, :], 0.0).then_inc(s_s12, 1)
                dve.wait_ge(s_s12, 1)
                dve.wait_ge(s_sT, 1)
                for b in range(B):
                    m = ROWS_P[b]
                    p4 = PS[b][0:m, 0:L * 2 * F].rearrange("p (l h f) -> p l h f", l=L, h=2)
                    for h in range(2):
                        last = v.tensor_copy(s12[h][0:m, b, :].rearrange("p (l f) -> p l f", f=F), p4[:, :, h, :])
                last.then_inc(s_s12, 1)
            with dve.Else():
                for k in range(3):
                    dve.wait_ge(s_y_out[k], 16 * len(range(k, B * L, 3)))
                dve.wait_ge(s_wr, 16)
                edges(2, 2)
                v.tensor_copy(t1[:, :, :], PS[2][:, :].rearrange("p (b c) -> p b c", b=B)).then_inc(s_s12, 1)
                v.tensor_copy(t2[:, :, :], PS[3][:, :].rearrange("p (b c) -> p b c", b=B)).then_inc(s_s12, 1)
            dve.wait_ge(s_s12, 2)
            chain(v.tensor_tensor(flat(t2), flat(t2), row(st2), ALU.mult))
            chain(v.tensor_tensor(t1[:, :, :], t1[:, :, :], t2[:, :, :], ALU.add))
            chain(v.tensor_tensor(t1[:, :, :], t1[:, :, :], x2n[:, :, :], ALU.add))
            layer_norm(t1, t1, 2).then_inc(s_res, 1)

        @block.tensor
        def _(pe):
            mm, tr = nc.tensor.matmul, nc.tensor.transpose
            pe.wait_ge(s_const, 16 * 6)
            pe.wait_ge(s_prep, 1)
            for g, (k, at, width) in enumerate(EDGE_T):
                if k == ROW:
                    pe.wait_ge(s_prep, 2)
                if g >= 2:
                    pe.wait_ge(s_tc, g - 1)
                for q in range(width // P):
                    last = tr(PS[g % 2][:, q * P:(q + 1) * P], raw[:, k, at + q * P:at + (q + 1) * P], ident[:, :])
                last.then_inc(s_tr, 1)
                if g == 1:
                    pe.wait_ge(s_rep, 1)
                    for k in range(3):
                        mm(PS[2][:, k * F:(k + 1) * F], wa_rep[:, k, :], ws_sb[:, :], start=True, stop=True)
                    mm(PS[2][0:KS, 64:65], ws_rep[:, :, :].rearrange("o s i -> o (s i)"), wa_sb[:, 0:1],
                       start=True, stop=True)
                    mm(PS[2][:, 192:192 + 4 * F], sel.rearrange("i l f -> i (l f)"),
                       w_lin.rearrange("i k o -> i (k o)"), start=True, stop=True)
                    tr(PS[3][0:BASES, 0:RELS], comp_sb, ident[0:RELS, 0:RELS]).then_inc(s_u, 1)
                if g == FIRSTS_AFTER:
                    pe.wait_ge(s_tc, len(EDGE_T) // 2)
                    for k, (at, n) in enumerate(((0, 512), (512, TILES - 512))):
                        for h in range(2):
                            d = dst_hl[:, h, :]
                            mm(PS[4 + k][:, 0:n], check[:, h, 0, :], d[:, at:at + n], start=(h == 0), stop=(h == 1))
                            mm(PS[6 + k][:, 0:n], check[:, h, 1, :], d[:, at:at + n], start=(h == 0), stop=False)
                            last = mm(PS[6 + k][:, 0:n], check[:, h, 2, :], d[:, at + 1:at + 1 + n],
                                      start=False, stop=(h == 1))
                    last.then_inc(s_first, 1)
                if g == 3:
                    pe.wait_ge(s_uc, 1)
                    mm(PS[3][0:RELS, 128:128 + F * F], compT, v_sb.rearrange("b i o -> b (i o)"),
                       start=True, stop=True).then_inc(s_t, 1)
            pe.wait_ge(s_dmin, 1)
            tr(PS[2][0:1, 128:256], tmp2[:, 2:3], ident[:, :]).then_inc(s_dminT, 1)

            def window_chunk(n, k):
                pe.wait_ge(s_prev, n + 1)
                for j in range(CW):
                    s, used = j % SLOTS_W, freed(n, j)
                    pe.wait_ge(s_oh, n * CW + j + 1)
                    if used is not None:
                        pe.wait_ge(s_cop, used + 1)
                    has_prev = not isinstance(n, int) or n * CW + j >= 1
                    o = PS[s][:, 0:W * NC]
                    for q in range(G):
                        last = mm(o, low(G * j + q), win_key[:, s, q, :], start=(q == 0),
                                  stop=(q == G - 1 and not has_prev))
                    if has_prev:
                        last = mm(PS[s][:, 0:NC], low(G * j - 1), win_prev[:, k, :, j],
                                  start=False, stop=True)
                    last.then_inc(s_win, 1)

            def dense(r):
                pe.wait_ge(s_xp, 4 * r + 4)
                if r == 0:
                    pe.wait_ge(s_cop, WINDOWS)

                def by_node(b):
                    pe.wait_ge(s_dca, r * len(range(0, NB, 2)) + b + 1)
                    pe.wait_ge(s_dcv, r * len(range(1, NB, 2)) + min(b + 1, len(range(1, NB, 2))))
                    m = ROWS_P[b]
                    for l in range(L):
                        at = b * P * L + l
                        last = tr(PS[b][0:m, l * 3 * F:(l + 1) * 3 * F],
                                  sum_t[0:3 * F, at:at + (m - 1) * L + 1:L], ident[0:3 * F, 0:3 * F])
                    last.then_inc(s_denT, 1)

                for q in range(NB):
                    n = min(512, NODES - q * 512)
                    for c in range(NC):
                        last = mm(PS[q][0:3 * F, 0:n], x_parts[:, c, :, :].rearrange("p s f -> p (s f)"),
                                  counts[:, c, q * 512:q * 512 + n], start=(c == 0), stop=(c == NC - 1))
                    last.then_inc(s_den, 1)
                    if q % 2 == 0 and q >= 2:
                        by_node(q // 2 - 1)
                by_node(B - 1)

            def edges(r, halves):
                for h in range(halves):
                    mm(PS[h][:, 0:HI], zeros[:, 0:P], zeros[:, 0:HI], start=True, stop=False)

                def chunk(n, k):
                    pe.wait_ge(s_ready[r], n + 1)
                    for j in range(CH):
                        for h in range(halves):
                            for q in range(3):
                                last = mm(PS[h][:, 0:HI], spread[:, k, j, 3 * h + q, :], oh_hi[:, k, j, 0:HI],
                                          start=False, stop=False)
                    last.then_inc(s_used[r], 1)

                with pe.Fori(0, CHUNKS, 2) as n:
                    chunk(n, 0)
                    chunk(n + 1, 1)
                for h in range(halves):
                    last = mm(PS[h][:, 0:HI], zeros[:, 0:P], zeros[:, 0:HI], start=False, stop=True)
                last.then_inc(s_agg[r], 1)
                pe.wait_ge(s_aggc[r], 1)
                for h in range(halves):
                    for b in range(B):
                        last = tr(PS[2 + h][:, b * P:(b + 1) * P], agg_sb[:, h, b * P:(b + 1) * P], ident[:, :])
                last.then_inc(s_aggT[r], 1)

            n_in = [0]

            def linear(k):
                n_in[0] += 1
                pe.wait_ge(s_in, n_in[0])
                for b in range(B):
                    last = tr(PS[4][:, b * P:(b + 1) * P], t1[:, b, :], ident[:, :])
                last.then_inc(s_inT, 1)
                pe.wait_ge(s_hT, n_in[0])
                for b in range(B):
                    last = mm(PS[3][:, b * P:(b + 1) * P], hT[:, b, :], kron[:, k, :], start=True, stop=True)
                last.then_inc(s_lin, 1)

            even = sorted_flag(pe)
            pe.wait_ge(s_zero, 1)
            with pe.If(even > 0):
                window_chunk(0, 0)
                with pe.Fori(1, WCHUNKS - 1, 2) as n:
                    window_chunk(n, 1)
                    window_chunk(n + 1, 0)
                dense(0)
            with pe.Else():
                edges(0, 1)
            pe.wait_ge(s_kron, 1)
            linear(0)
            linear(1)
            with pe.If(even > 0):
                dense(1)
            with pe.Else():
                edges(1, 1)
            linear(2)
            linear(3)
            pe.wait_ge(s_xs, 1)
            for g in range(B * L // 4):
                if g >= 2:
                    pe.wait_ge(s_xTc, g - 1)
                for q in range(4):
                    c = 4 * g + q
                    last = tr(PS[g % 2][:, :].bitcast(BF16)[0:KS, q * P:(q + 1) * P],
                              xs[:, c, :, :].rearrange("p s f -> p (s f)"), ident_bf[:, :])
                last.then_inc(s_xT, 1)
            pe.wait_ge(s_xTc, B * L // 4)
            pe.wait_ge(s_attr_used, ATTR_N)
            for b in range(EDGE_BLOCKS):
                last = tr(PS[b // 4][:, (b % 4) * P:(b % 4 + 1) * P], logit_raw[:, b * P:(b + 1) * P], ident[:, :])
            last.then_inc(s_lT, 1)
            for c in range(B * L):
                m = ROWS_P[c // L]
                if c >= 2:
                    pe.wait_ge(s_ya, c - 1)
                    pe.wait_ge(s_yv, c - 1)
                for q in range(3):
                    last = mm(PS[2 + 3 * (c % 2) + q][0:m, 0:YBANK], xsT[:, c, 0:m],
                              w_stack[:, q * YBANK:(q + 1) * YBANK], start=True, stop=True)
                last.then_inc(s_y, 1)
            pe.wait_ge(s_logit, 2)
            pe.wait_ge(s_ya, B * L)
            pe.wait_ge(s_yv, B * L)

            def gather_window(n, k, w):
                b = w % PAIRS
                if w == 0:
                    pe.wait_ge(s_ohT, n + 1)
                    pe.wait_ge(s_type, n + 1)
                again = w >= PAIRS or not isinstance(n, int) or n >= 1
                if again:
                    pe.wait_ge(s_mask, n * QW + w - PAIRS + 1)
                for q in range(G):
                    t = G * w + q
                    for i, (c, s) in enumerate(GATHERS):
                        h = len(range(c, NC, KC))
                        mm(PS[b][:, q * HC * FX:(q * HC + h) * FX], src_oh[:, k, c, t * P:(t + 1) * P],
                           x2_parts[:, 0:h, c, s, :], start=(i == 0), stop=(i == len(GATHERS) - 1))
                if again:
                    pe.wait_ge(s_gc, n * QW + w - PAIRS + 1)
                for q in range(G):
                    t = G * w + q
                    for s in range(3):
                        last = mm(PS[PAIRS + b][:, q * F * F:(q + 1) * F * F], type_oh[0:RELS, k, t * P:(t + 1) * P],
                                  w_parts[:, s, :], start=(s == 0), stop=(s == 2))
                last.then_inc(s_g, 1)

            def sum_windows(n, k, windows):
                if windows[0] == 0:
                    pe.wait_ge(s_msg, n + 1)
                    pe.wait_ge(s_c3, n * CW + 1)
                for j in windows:
                    for q in range(G):
                        t = G * j + q
                        last = mm(PS[2 * PAIRS][0:2 * F, j * W:(j + 1) * W], mess[:, k, t, 0:2 * F],
                                  loc_oh[:, k, t, :], start=(q == 0), stop=(q == G - 1))
                if windows[-1] == CW - 1:
                    last.then_inc(s_scat, 1)

            def gather_and_sum(n, k, ahead=True):
                for w in range(PAIRS, QW):
                    gather_window(n, k, w)
                    if not isinstance(n, int) or n >= 1:
                        i, of = w - PAIRS, QW - PAIRS
                        sum_windows(n - 1, 1 - k, range(i * CW // of, (i + 1) * CW // of))
                if ahead:
                    for w in range(PAIRS):
                        gather_window(n + 1, 1 - k, w)

            with pe.If(even > 0):
                pe.wait_ge(s_parts, 7)
                pe.wait_ge(s_wr, 16)
                for w in range(PAIRS):
                    gather_window(0, 0, w)
                gather_and_sum(0, 0)
                gather_and_sum(1, 1)
                with pe.Fori(2, WCHUNKS - 1, 2) as n:
                    gather_and_sum(n, 0)
                    gather_and_sum(n + 1, 1)
                gather_and_sum(WCHUNKS - 1, 0, ahead=False)
                sum_windows(WCHUNKS - 1, 0, range(CW))
                pe.wait_ge(s_c3, WINDOWS + 1)
                for b in range(B):
                    m = ROWS_P[b]
                    for l in range(L):
                        at = b * P * L + l
                        last = tr(PS[b][0:m, l * 2 * F:(l + 1) * 2 * F],
                                  sums[:, at:at + (m - 1) * L + 1:L], ident[0:2 * F, 0:2 * F])
                last.then_inc(s_sT, 1)
            with pe.Else():
                edges(2, 2)


EDGE_COLS = EDGE_BLOCKS * P
GATHERS = [(0, 0)] + [(c, s) for c in range(1, KC) for s in range(3)] + [(0, 1), (0, 2)]
W_PARTS = (0, 1, 2, 0, 1, 0)
FIRSTS_AFTER = 5
NO_KEY = 2000
ATTR_E = 16
ATTR_N = EDGE_COLS // ATTR_E
EDGE_T = [(k, at, min(512, EDGE_COLS - at)) for k in (2, 3, 0, 1) for at in range(0, EDGE_COLS, 512)]


def attr_rows(attr, sb, b, q):
    tiles = P if b < FULL_EB else LAST_T
    top = b * P * P
    yield (attr[top:top + tiles * P, :].rearrange("(t e) f -> t (e f)", e=P)[
        :, q * ATTR_E * F:(q + 1) * ATTR_E * F], sb[0:tiles, :])
    left = min(ATTR_E, LAST_E - q * ATTR_E)
    if b == FULL_EB and left > 0:
        at = top + tiles * P + q * ATTR_E
        yield attr[at:at + left, :].rearrange("(a e) f -> a (e f)", a=1), sb[tiles:tiles + 1, 0:left * F]


_INS = ['x', 'src', 'dst', 'edge_attr_16', 'edge_type_90', 'L0_gnn_eps1', 'L0_gnn_w1a', 'L0_gnn_b1a',
        'L0_gnn_w1b', 'L0_gnn_b1b', 'L0_gnn_eps2', 'L0_gnn_w2a', 'L0_gnn_b2a', 'L0_gnn_w2b',
        'L0_gnn_b2b', 'L1_gnn_Ws', 'L1_gnn_Wa', 'L1_gnn_weight', 'L1_gnn_w_comp']


def shape_constants():
    slots = np.zeros((KS, 3), np.float32)
    for s, part_of_w in enumerate(W_PARTS):
        slots[s * F:(s + 1) * F, part_of_w] = 1
    check = np.zeros((P, 3, P), np.float16)
    check[0, 0, :] = 1
    check[np.arange(P), 1, np.arange(P)] = -1
    check[np.arange(1, P), 1, np.arange(P - 1)] = 1
    check[0, 2, P - 1] = 1
    return {
        "ident": np.eye(P, dtype=np.float32),
        "iota_hi": np.arange(HI).astype(np.float16),
        "lane_l": np.repeat(np.arange(L), F).astype(np.float16),
        "slots": slots,
        "check": np.stack([L * check, check], 1),
        "lane": np.concatenate([np.arange(P)[:, None] + P * np.arange(KC)[None, :],
                                np.arange(P)[:, None] // F == np.arange(L)[None, :],
                                -np.arange(P)[:, None], np.ones((P, 1))], 1).astype(np.float32),
    }


def kernel(**inputs):
    import concourse.bacc as _bacc
    from concourse.bass_utils import run_bass_kernel_spmd as _run

    nc = _bacc.Bacc("TRN2", target_bir_lowering=False, num_devices=1)
    arrays, args = {}, []
    for name in _INS:
        a = np.ascontiguousarray(inputs[name])
        if a.ndim == 0 or name.startswith("L0_gnn_eps"):
            a = a.reshape(1)
        arrays[f"in_{name}"] = a
        args.append(nc.dram_tensor(f"in_{name}", a.shape, mybir.dt.from_np(a.dtype), kind="ExternalInput").ap())
    for name, a in shape_constants().items():
        arrays[f"const_{name}"] = a
        args.append(nc.dram_tensor(f"const_{name}", a.shape, mybir.dt.from_np(a.dtype), kind="ExternalInput").ap())
    args.append(nc.dram_tensor("out_0", (NODES, F), FP32, kind="ExternalOutput").ap())
    build_gnn(nc, *args)
    r = _run(nc, [arrays], core_ids=[0])
    return r.results[0]["out_0"]
```
